# Optimizing a Trainium2 kernel written in Bass

```python
import numpy as np
import jax
import jax.numpy as jnp

def _softmax(x, axis=-1):
    return jax.nn.softmax(x, axis=axis)

def _gelu(x):
    return jax.nn.gelu(x, approximate=True)

def _silu(x):
    return jax.nn.silu(x)

def _sigmoid(x):
    return jax.nn.sigmoid(x)

def _layernorm(x, axis=-1, eps=1e-05):
    m = jnp.mean(x, axis=axis, keepdims=True)
    v = jnp.var(x, axis=axis, keepdims=True)
    return (x - m) / jnp.sqrt(v + eps)

def _scatter_add(tgt, idx, src, axis=0):
    return tgt.at[idx].add(src)

def _segment_sum(src, seg, n):
    return jax.ops.segment_sum(src, seg, n)
kernel_name = 'mk_recurrent_d1_jaxref_r4_53a5fc'

def setup_inputs(seed: int=0):
    np.random.seed(seed)
    _w = jnp.asarray

    def _L0_attn_setup():
        import jax, jax.numpy as jnp
        import numpy as np
        B, S, HID = (2, 512, 512)
        H, D, K = (16, 128, 4)
        ROPE_BASE = 1000000.0
        EPS_NORM = 1e-06

        def _silu(u):
            return u * jax.nn.sigmoid(u)

        def _causal_dwconv(x_bsc, w_ck):
            C, Kw = w_ck.shape
            y = jax.lax.conv_general_dilated(x_bsc.transpose(0, 2, 1), w_ck[:, None, :], (1,), [(Kw - 1, 0)], dimension_numbers=('NCH', 'OIH', 'NCH'), feature_group_count=C)
            return y.transpose(0, 2, 1)

        def _lag(u, s):
            if s == 0:
                return u
            pad = [(0, 0), (s, 0)] + [(0, 0)] * (u.ndim - 2)
            return jnp.pad(u, pad)[:, :u.shape[1]]
        key = jax.random.key(seed)
        ks = jax.random.split(key, 12)
        p = lambda k, shape: jax.random.normal(k, shape, jnp.float32) * 0.02
        x = jax.random.normal(ks[0], (B, S, HID), jnp.float32)
        return {'x': x, 'Wq': p(ks[1], (HID, H * D)), 'Wk': p(ks[2], (HID, H * D)), 'Wv': p(ks[3], (HID, H * D)), 'Wz': p(ks[4], (HID, H * D)), 'Wa': p(ks[5], (HID, H)), 'Wb': p(ks[6], (HID, H)), 'conv_q_w': p(ks[7], (H * D, K)), 'conv_k_w': p(ks[8], (H * D, K)), 'conv_v_w': p(ks[9], (H * D, K)), 'norm_w': jnp.ones((H * D,), jnp.float32), 'Wout': p(ks[10], (H * D, HID))}
    _L0_attn_in = _L0_attn_setup()

    def _L0_ffn_setup():
        import jax, jax.numpy as jnp
        import numpy as np

        @jax.custom_vjp
        def ste_sign(x):
            return jnp.sign(x)

        def _ste_fwd(x):
            return (jnp.sign(x), None)

        def _ste_bwd(_, g):
            return (g,)
        ste_sign.defvjp(_ste_fwd, _ste_bwd)
        D_MODEL = 512
        D_HIDDEN = 2048
        key = jax.random.key(seed)
        k_x, k_up, k_dn = jax.random.split(key, 3)
        x = jax.random.normal(k_x, (2, 512, D_MODEL), dtype=jnp.float32)
        up_weight = jax.random.normal(k_up, (D_HIDDEN, D_MODEL), dtype=jnp.float32) * 0.02
        down_weight = jax.random.normal(k_dn, (D_MODEL, D_HIDDEN), dtype=jnp.float32) * 0.02
        up_scale = jnp.ones((D_HIDDEN,), dtype=jnp.float32)
        down_scale = jnp.ones((D_MODEL,), dtype=jnp.float32)
        output_scale = jnp.ones((1,), dtype=jnp.float32)
        return {'x': x, 'up_weight': up_weight, 'down_weight': down_weight, 'up_scale': up_scale, 'down_scale': down_scale, 'output_scale': output_scale}
    _L0_ffn_in = _L0_ffn_setup()
    _d = {'L0_attn_x': _L0_attn_in['x'], 'L0_attn_Wq': _L0_attn_in['Wq'], 'L0_attn_Wk': _L0_attn_in['Wk'], 'L0_attn_Wv': _L0_attn_in['Wv'], 'L0_attn_Wz': _L0_attn_in['Wz'], 'L0_attn_Wa': _L0_attn_in['Wa'], 'L0_attn_Wb': _L0_attn_in['Wb'], 'L0_attn_conv_q_w': _L0_attn_in['conv_q_w'], 'L0_attn_conv_k_w': _L0_attn_in['conv_k_w'], 'L0_attn_conv_v_w': _L0_attn_in['conv_v_w'], 'L0_attn_norm_w': _L0_attn_in['norm_w'], 'L0_attn_Wout': _L0_attn_in['Wout'], 'L0_ffn_up_weight': _L0_ffn_in['up_weight'], 'L0_ffn_down_weight': _L0_ffn_in['down_weight'], 'L0_ffn_up_scale': _L0_ffn_in['up_scale'], 'L0_ffn_down_scale': _L0_ffn_in['down_scale'], 'L0_ffn_output_scale': _L0_ffn_in['output_scale']}
    _x0 = _d['L0_attn_x']
    _d['L0_attn_x'] = jax.random.normal(jax.random.fold_in(jax.random.key(seed), 1), (1, 2048, 512), dtype=_x0.dtype)
    del _x0
    return _d

def reference(L0_attn_x, L0_attn_Wq, L0_attn_Wk, L0_attn_Wv, L0_attn_Wz, L0_attn_Wa, L0_attn_Wb, L0_attn_conv_q_w, L0_attn_conv_k_w, L0_attn_conv_v_w, L0_attn_norm_w, L0_attn_Wout, L0_ffn_up_weight, L0_ffn_down_weight, L0_ffn_up_scale, L0_ffn_down_scale, L0_ffn_output_scale):

    def _L0_attn_ref(x, Wq, Wk, Wv, Wz, Wa, Wb, conv_q_w, conv_k_w, conv_v_w, norm_w, Wout):
        import jax, jax.numpy as jnp
        import numpy as np
        B, S, HID = (2, 512, 512)
        H, D, K = (16, 128, 4)
        ROPE_BASE = 1000000.0
        EPS_NORM = 1e-06

        def _silu(u):
            return u * jax.nn.sigmoid(u)

        def _causal_dwconv(x_bsc, w_ck):
            C, Kw = w_ck.shape
            y = jax.lax.conv_general_dilated(x_bsc.transpose(0, 2, 1), w_ck[:, None, :], (1,), [(Kw - 1, 0)], dimension_numbers=('NCH', 'OIH', 'NCH'), feature_group_count=C)
            return y.transpose(0, 2, 1)

        def _lag(u, s):
            if s == 0:
                return u
            pad = [(0, 0), (s, 0)] + [(0, 0)] * (u.ndim - 2)
            return jnp.pad(u, pad)[:, :u.shape[1]]
        Bc, Sc, _ = x.shape
        q = _silu(x @ Wq)
        k = _silu(x @ Wk)
        v = _silu(x @ Wv)
        z = x @ Wz
        a = x @ Wa
        b = x @ Wb
        q = _causal_dwconv(q, conv_q_w)
        k = _causal_dwconv(k, conv_k_w)
        v = _causal_dwconv(v, conv_v_w)
        q = q.reshape(Bc, Sc, H, D)
        k = k.reshape(Bc, Sc, H, D)
        v = v.reshape(Bc, Sc, H, D)
        inv = 1.0 / ROPE_BASE ** (jnp.arange(0, D, 2, dtype=jnp.float32) / D)
        fr = jnp.arange(Sc, dtype=jnp.float32)[:, None] * inv[None, :]
        cos = jnp.concatenate([jnp.cos(fr), jnp.cos(fr)], -1)[None, :, None, :]
        sin = jnp.concatenate([jnp.sin(fr), jnp.sin(fr)], -1)[None, :, None, :]

        def rot_half(u):
            u1, u2 = jnp.split(u, 2, axis=-1)
            return jnp.concatenate([-u2, u1], axis=-1)
        q = q * cos + rot_half(q) * sin
        k = k * cos + rot_half(k) * sin
        q = q / jnp.maximum(jnp.linalg.norm(q, axis=-1, keepdims=True), 1e-12)
        k = k / jnp.maximum(jnp.linalg.norm(k, axis=-1, keepdims=True), 1e-12)
        scale = 1.0 / D ** 0.5
        out = jnp.zeros_like(v)
        for s in range(K):
            k_s = _lag(k, s)
            v_s = _lag(v, s)
            a_s = _lag(a, s)
            attn = jnp.einsum('bshd,bshd->bsh', q, k_s) * scale
            gate = jax.nn.sigmoid(a_s * b)
            out = out + (attn * gate)[..., None] * v_s
        out = out.reshape(Bc, Sc, H * D)
        rms = jax.lax.rsqrt(jnp.mean(out * out, axis=-1, keepdims=True) + EPS_NORM)
        out = out * rms * norm_w * _silu(z)
        return out @ Wout

    def _L0_ffn_ref(x, up_weight, down_weight, up_scale, down_scale, output_scale):
        import jax, jax.numpy as jnp
        import numpy as np

        @jax.custom_vjp
        def ste_sign(x):
            return jnp.sign(x)

        def _ste_fwd(x):
            return (jnp.sign(x), None)

        def _ste_bwd(_, g):
            return (g,)
        ste_sign.defvjp(_ste_fwd, _ste_bwd)
        D_MODEL = 512
        D_HIDDEN = 2048
        up_w = ste_sign(up_weight)
        down_w = ste_sign(down_weight)
        hidden = jnp.einsum('bsd,hd->bsh', x, up_w) * up_scale
        hidden = jax.nn.relu(hidden)
        out = jnp.einsum('bsh,dh->bsd', hidden, down_w) * down_scale
        return out * output_scale
    x = L0_attn_x
    xn = _layernorm(x, axis=-1)
    s = _L0_attn_ref(xn, L0_attn_Wq, L0_attn_Wk, L0_attn_Wv, L0_attn_Wz, L0_attn_Wa, L0_attn_Wb, L0_attn_conv_q_w, L0_attn_conv_k_w, L0_attn_conv_v_w, L0_attn_norm_w, L0_attn_Wout)
    g = _silu(_L0_ffn_ref(xn, L0_ffn_up_weight, L0_ffn_down_weight, L0_ffn_up_scale, L0_ffn_down_scale, L0_ffn_output_scale))
    x = x + s * g
    return x

_drawn_inputs = setup_inputs


def setup_inputs(seed=0):
    import zlib

    import numpy as np

    out = dict(_drawn_inputs(seed))
    spreads = {'L0_attn_norm_w': (1.0, 0.2),
     'L0_ffn_up_scale': (1.0, 0.2),
     'L0_ffn_down_scale': (1.0, 0.2)}
    factors = {}
    for name, (base, spread) in spreads.items():
        noise = np.random.default_rng([zlib.crc32(name.encode()), seed]).standard_normal(out[name].shape)
        drawn = base * np.exp(spread * noise) if base else spread * noise
        out[name] = jnp.asarray(drawn.astype(out[name].dtype))
    for name, factor in factors.items():
        out[name] = (out[name] * factor).astype(out[name].dtype)
    return out
```

```python
import concourse.bass as bass
from concourse import mybir
from contextlib import ExitStack


def gated_recurrent_block_kernel(
    nc: bass.Bass,
    x: bass.AP,
    wq: bass.AP,
    wk: bass.AP,
    wv: bass.AP,
    wz: bass.AP,
    wa: bass.AP,
    wb: bass.AP,
    conv_q: bass.AP,
    conv_k: bass.AP,
    conv_v: bass.AP,
    norm_w: bass.AP,
    wout: bass.AP,
    up_t: bass.AP,
    down_t: bass.AP,
    up_scale: bass.AP,
    down_scale: bass.AP,
    output_scale: bass.AP,
    masks: bass.AP,
    rope_cos: bass.AP,
    rope_sin: bass.AP,
    out: bass.AP,
):
    fp32 = mybir.dt.float32
    f32r = mybir.dt.float32r
    ALU = mybir.AluOpType
    ACT = mybir.ActivationFunctionType

    P = 128
    S, HID = x.shape
    KT = HID // P
    HD = wq.shape[1]
    D = P
    H = HD // D
    FH = up_t.shape[1]
    FT = FH // P
    CH = 512
    G = S // CH
    BC = CH // P
    NB = S // P
    LAGS = 4
    HALO = LAGS - 1
    TAPS = 4
    BW = P + LAGS
    AB = 2 * H
    LN_EPS, RMS_EPS, NORM_FLOOR = 1e-5, 1e-6, 1e-24
    SCALE = float(D) ** -0.5

    C_ID, C_SEL, C_HALO, C_BAND, C_PER = 0, P, 2 * P, 3 * P, 3 * P + BW

    o_scratch = nc.dram_tensor("o_scratch", [HD, S], fp32).ap()

    def wait(eng, sem, count):
        if isinstance(count, int) and count <= 0:
            return
        eng.wait_ge(sem, count)

    top = ExitStack()
    with top:
        def sb(name, shape, dt=fp32, at=top):
            return at.enter_context(nc.sbuf_tensor(name, shape, dt))

        def sem(name, at=top):
            return at.enter_context(nc.semaphore(name))

        const = sb("const", [P, masks.shape[1]])
        neg_half = sb("neg_half", [P, 2 * NB])
        x_hi = sb("x_hi", [P, KT, S], f32r)
        x_lo = sb("x_lo", [P, KT, S], f32r)
        sq_sum = sb("sq_sum", [P, S])
        nw_sb = sb("nw_sb", [P, H])
        us_sb = sb("us_sb", [P, FT])
        ident = const[:, C_ID:C_ID + P]
        sel_own = const[:, C_SEL:C_SEL + P]
        sel_next = const[:, C_HALO:C_HALO + P]
        band = const[:, C_BAND:C_BAND + BW]
        period = const[:, C_PER:C_PER + LAGS]

        banks = [top.enter_context(nc.psum_tensor(f"bank{i}", [P, 512], fp32)) for i in range(4)]
        pair = top.enter_context(nc.psum_tensor("bank45", [P, 1024], fp32))
        banks2 = [top.enter_context(nc.psum_tensor(f"bank{i}", [P, 512], fp32)) for i in (6, 7)]

        att = ExitStack()
        with att:
            cw = {n: sb(f"cw_{n}", [P, H * TAPS], at=att) for n in "qkv"}
            gate0 = sb("gate0", [P, NB, H * LAGS], at=att)
            raw = {n: sb(f"raw_{n}", [P, KT, D], at=att) for n in "qkvz"}
            w_hi = {n: sb(f"whi_{n}", [P, KT, D], f32r, at=att) for n in "qkvz"}
            w_lo = {n: sb(f"wlo_{n}", [P, KT, D], f32r, at=att) for n in "qkvz"}
            w_dram = {"q": wq, "k": wk, "v": wv, "z": wz}
            raw_in = {n: sem(f"raw_in_{n}", att) for n in "qkvz"}
            whi_done = {n: sem(f"whi_done_{n}", att) for n in "qkvz"}
            wlo_done = {n: sem(f"wlo_done_{n}", att) for n in "qkvz"}

            def w_slice(n, h):
                return w_dram[n].rearrange("(t p) n -> p t n", p=P)[:, :, bass.ds(h * D, D)]

            prologue(nc, locals())
            attention(nc, locals())

        ffn_and_output(nc, locals())


def prologue(nc, env):
    (fp32, f32r, ALU, ACT, P, S, HID, KT, H, CH, G, BC, NB, LAGS, AB, SCALE, LN_EPS, sb, sem, wait) = (
        env[n] for n in ("fp32", "f32r", "ALU", "ACT", "P", "S", "HID", "KT", "H", "CH", "G", "BC", "NB",
                         "LAGS", "AB", "SCALE", "LN_EPS", "sb", "sem", "wait"))
    (const, neg_half, x_hi, x_lo, sq_sum, ident, sel_own, sel_next, period, banks, pair, cw, gate0, raw,
     w_hi, w_lo, raw_in, whi_done, wlo_done, w_slice) = (
        env[n] for n in ("const", "neg_half", "x_hi", "x_lo", "sq_sum", "ident", "sel_own", "sel_next",
                         "period", "banks", "pair", "cw", "gate0", "raw", "w_hi", "w_lo", "raw_in",
                         "whi_done", "wlo_done", "w_slice"))
    with ExitStack() as ctx:
        xt = sb("xt", [P, NB, HID], at=ctx)
        stats = sb("stats", [P, NB, 6], at=ctx)
        mean_var = sb("mean_var", [P, NB, 2], at=ctx)
        rstd = sb("rstd", [P, NB], at=ctx)
        ab_raw = sb("ab_raw", [P, KT, P], at=ctx)
        ab_hi = sb("ab_hi", [P, KT, P], f32r, at=ctx)
        ab_lo = sb("ab_lo", [P, KT, P], f32r, at=ctx)
        ab_t = sb("ab_t", [AB, S], at=ctx)
        ab = sb("ab", [P, NB, AB], at=ctx)
        bx = sb("bx", [P, NB + 1, H, LAGS], at=ctx)
        const_in = sem("const_in", ctx)
        x_in = [sem(f"x_in{g}", ctx) for g in range(G)]
        small_in = sem("small_in", ctx)
        zeroed = sem("zeroed", ctx)
        ab_in = sem("ab_in", ctx)
        stats_done = sem("stats_done", ctx)
        moments = sem("moments", ctx)
        var_eps = sem("var_eps", ctx)
        rstd_done = sem("rstd_done", ctx)
        normed = sem("normed", ctx)
        turned = sem("turned", ctx)
        hi_done = sem("hi_done", ctx)
        lo_done = sem("lo_done", ctx)
        abw_hi = sem("abw_hi", ctx)
        abw_lo = sem("abw_lo", ctx)
        ab_proj = sem("ab_proj", ctx)
        abt_done = sem("abt_done", ctx)
        ab_turned = sem("ab_turned", ctx)
        ab_done = sem("ab_done", ctx)
        bx_done = sem("bx_done", ctx)
        picked = sem("picked", ctx)
        prod_done = sem("prod_done", ctx)
        tanh_done = sem("tanh_done", ctx)
        gate_done = sem("gate_done", ctx)
        block = ctx.enter_context(nc.Block())

        @block.sync
        def _(sp):
            for g in range(G):
                sp.dma_start(xt[:, g * BC:(g + 1) * BC, :],
                             env["x"].rearrange("(b p) d -> p b d", p=P)[:, g * BC:(g + 1) * BC, :]
                             ).then_inc(x_in[g], 16)
                if g == 0:
                    sp.dma_start(const[:, :], env["masks"]).then_inc(const_in, 16)
            wait(sp, zeroed, 1)
            sp.dma_start(ab_raw[:, :, 0:H], env["wa"].rearrange("(t p) n -> p t n", p=P)).then_inc(ab_in, 16)
            sp.dma_start(ab_raw[:, :, H:AB], env["wb"].rearrange("(t p) n -> p t n", p=P)).then_inc(ab_in, 16)
            for n in "qkvz":
                sp.dma_start(raw[n][:, :, :], w_slice(n, 0)).then_inc(raw_in[n], 16)
            for n in "qkv":
                sp.dma_start(cw[n][:, :], env[f"conv_{n}"]).then_inc(small_in, 16)
            sp.dma_start(env["nw_sb"][:, :], env["norm_w"]).then_inc(small_in, 16)
            sp.dma_start(env["us_sb"][:, :], env["up_scale"]).then_inc(small_in, 16)
            sp.wait_ge(small_in, 16 * 5)

        @block.gpsimd
        def _(pool):
            nc.gpsimd.memset(ab_raw[:, :, :], 0.0).then_inc(zeroed, 1)
            nc.gpsimd.memset(neg_half[:, :], -0.5).then_inc(zeroed, 1)
            nc.gpsimd.memset(bx[:, NB, :, :], 0.0).then_inc(zeroed, 1)
            nc.gpsimd.memset(sq_sum[:, :], 0.0).then_inc(zeroed, 1)
            pool.wait_ge(zeroed, 4)
            for g in range(G):
                part = slice(g * BC, (g + 1) * BC)
                pool.wait_ge(moments, (g + 1) * BC)
                nc.gpsimd.tensor_scalar(rstd[:, part], mean_var[:, part, 1], LN_EPS, None, ALU.add
                                        ).then_inc(var_eps, 1)
                pool.wait_ge(var_eps, g + 1)
                nc.gpsimd.tensor_tensor(rstd[:, part], rstd[:, part], neg_half[:, part], ALU.pow
                                        ).then_inc(rstd_done, 1)
            for n in "qkvz":
                pool.wait_ge(whi_done[n], 1)
                nc.gpsimd.tensor_tensor(w_lo[n][:, :, :], raw[n][:, :, :], w_hi[n][:, :, :].bitcast(fp32),
                                        ALU.subtract).then_inc(wlo_done[n], 1)

        @block.vector
        def _(dve):
            for b in range(NB):
                if b % BC == 0:
                    dve.wait_ge(x_in[b // BC], 16)
                nc.vector.bn_stats(stats[:, b, :], xt[:, b, :]).then_inc(stats_done, 1)
            for b in range(NB):
                dve.wait_ge(stats_done, b + 1)
                nc.vector.bn_aggr(mean_var[:, b, :], stats[:, b, :]).then_inc(moments, 1)
            dve.wait_ge(abw_hi, 1)
            nc.vector.tensor_tensor(ab_lo[:, :, :], ab_raw[:, :, :], ab_hi[:, :, :].bitcast(fp32),
                                    ALU.subtract).then_inc(abw_lo, 1)

            def normalize(b):
                dve.wait_ge(rstd_done, b // BC + 1)
                nc.vector.tensor_scalar(xt[:, b, :], xt[:, b, :], mean_var[:, b, 0:1], rstd[:, b:b + 1],
                                        ALU.subtract, ALU.mult).then_inc(normed, 1)

            normalize(0)
            normalize(1)
            for b in range(NB):
                if b + 2 < NB:
                    normalize(b + 2)
                dve.wait_ge(hi_done, b + 1)
                nc.vector.tensor_tensor(
                    x_lo[:, :, b * P:(b + 1) * P], banks[b % 4][:, :].rearrange("p (t n) -> p t n", t=KT),
                    x_hi[:, :, b * P:(b + 1) * P].bitcast(fp32), ALU.subtract).then_inc(lo_done, 1)
            dve.wait_ge(ab_turned, NB)
            nc.vector.tensor_copy(ab[:, :, :], pair[:, 0:NB * AB].rearrange("p (b n) -> p b n", b=NB)
                                  ).then_inc(ab_done, 1)
            dve.wait_ge(ab_done, 1)
            dve.wait_ge(const_in, 16)
            for r in range(LAGS):
                nc.vector.tensor_scalar(bx[:, 0:NB, :, r], ab[:, :, H:AB], period[:, r:r + 1], None, ALU.mult
                                        ).then_inc(bx_done, 1)
            half = NB // 2
            for i in range(2):
                dve.wait_ge(picked, i + 1)
                nc.vector.tensor_tensor(
                    gate0[:, i * half:(i + 1) * half, :].rearrange("p b (h r) -> p b h r", h=H),
                    banks[i][:, :].rearrange("p (b h r) -> p b h r", b=half, h=H),
                    ab[:, i * half:(i + 1) * half, 0:H][:, :, :, None].broadcast_to([P, half, H, LAGS]),
                    ALU.mult).then_inc(prod_done, 1)
            for i in range(2):
                part = gate0[:, i * half:(i + 1) * half, :]
                dve.wait_ge(tanh_done, i + 1)
                nc.vector.tensor_scalar(part, part, 1.0, 0.5 * SCALE, ALU.add, ALU.mult).then_inc(gate_done, 1)

        @block.scalar
        def _(act):
            act.wait_ge(ab_in, 32)
            nc.scalar.activation(ab_hi[:, :, :], ab_raw[:, :, :], ACT.Copy).then_inc(abw_hi, 1)
            for n in "qkvz":
                act.wait_ge(raw_in[n], 16)
                nc.scalar.activation(w_hi[n][:, :, :], raw[n][:, :, :], ACT.Copy).then_inc(whi_done[n], 1)
            for b in range(NB):
                act.wait_ge(turned, b + 1)
                nc.scalar.activation(x_hi[:, :, b * P:(b + 1) * P],
                                     banks[b % 4][:, :].rearrange("p (t n) -> p t n", t=KT),
                                     ACT.Copy).then_inc(hi_done, 1)
            for g in range(G):
                act.wait_ge(ab_proj, g + 1)
                nc.scalar.activation(ab_t[:, g * CH:(g + 1) * CH], banks[g][0:AB, :], ACT.Copy
                                     ).then_inc(abt_done, 1)
            half = NB // 2
            for i in range(2):
                part = gate0[:, i * half:(i + 1) * half, :]
                act.wait_ge(prod_done, i + 1)
                nc.scalar.activation(part, part, ACT.Tanh, scale=0.5).then_inc(tanh_done, 1)

        @block.tensor
        def _(pe):
            pe.wait_ge(const_in, 16)
            for b in range(NB):
                pe.wait_ge(normed, b + 1)
                wait(pe, lo_done, b - 3)
                for t in range(KT):
                    last = nc.tensor.transpose(banks[b % 4][:, t * P:(t + 1) * P],
                                               xt[:, b, t * P:(t + 1) * P], ident)
                last.then_inc(turned, 1)
            pe.wait_ge(abw_lo, 1)
            for g in range(G):
                pe.wait_ge(lo_done, NB)
                cols = slice(g * CH, (g + 1) * CH)
                terms = [(w, part, t) for w, part in ((ab_hi, x_hi), (ab_lo, x_hi), (ab_hi, x_lo))
                         for t in range(KT)]
                for i, (w, part, t) in enumerate(terms):
                    last = nc.tensor.matmul(banks[g][:, :], w[:, t, :], part[:, t, cols],
                                            start=(i == 0), stop=(i == len(terms) - 1))
                last.then_inc(ab_proj, 1)
            for b in range(NB):
                pe.wait_ge(abt_done, b // BC + 1)
                nc.tensor.transpose(pair[:, b * AB:(b + 1) * AB], ab_t[:, b * P:(b + 1) * P],
                                    ident[0:AB, 0:AB]).then_inc(ab_turned, 1)
            pe.wait_ge(bx_done, LAGS)
            pe.wait_ge(zeroed, 4)
            half = NB // 2
            for i in range(2):
                own = bx[:, i * half:(i + 1) * half, :, :].rearrange("p b h r -> p (b h r)")
                after = bx[:, i * half + 1:(i + 1) * half + 1, :, :].rearrange("p b h r -> p (b h r)")
                nc.tensor.matmul(banks[i][:, :], sel_own, own, start=True, stop=False)
                nc.tensor.matmul(banks[i][:, :], sel_next, after, start=False, stop=True).then_inc(picked, 1)


def attention(nc, env):
    (fp32, f32r, ALU, ACT, P, S, KT, H, D, CH, G, BC, NB, LAGS, HALO, TAPS, BW, NORM_FLOOR, sb, sem, wait) = (
        env[n] for n in ("fp32", "f32r", "ALU", "ACT", "P", "S", "KT", "H", "D", "CH", "G", "BC", "NB", "LAGS",
                         "HALO", "TAPS", "BW", "NORM_FLOOR", "sb", "sem", "wait"))
    (neg_half, x_hi, x_lo, sq_sum, ident, sel_own, sel_next, band, period, banks, pair, banks2, cw, gate0,
     raw, w_hi, w_lo, raw_in, whi_done, wlo_done, w_slice, nw_sb, o_scratch) = (
        env[n] for n in ("neg_half", "x_hi", "x_lo", "sq_sum", "ident", "sel_own", "sel_next", "band",
                         "period", "banks", "pair", "banks2", "cw", "gate0", "raw", "w_hi", "w_lo", "raw_in",
                         "whi_done", "wlo_done", "w_slice", "nw_sb", "o_scratch"))
    NC = H * G
    HALF = D // 2
    with ExitStack() as ctx:
        cos = sb("cos", [P, S], at=ctx)
        sin = sb("sin", [P, S], at=ctx)
        u = {n: sb(f"u_{n}", [P, 2, CH + HALO], at=ctx) for n in "qkv"}
        y = {n: sb(f"y_{n}", [P, 2, CH], at=ctx) for n in "qkv"}
        swapped = {n: sb(f"swapped_{n}", [P, 2, CH], at=ctx) for n in "qk"}
        rot = {"q": sb("rot_q", [P, S + LAGS], at=ctx), "k": sb("rot_k", [P, S], at=ctx)}
        norms = sb("norms", [P, 2, 2 * BC], at=ctx)
        rnorm = sb("rnorm", [P, 2, 2 * BC], at=ctx)
        rq_x = sb("rq_x", [P, (NB + 1), LAGS], at=ctx)
        gate_k = sb("gate_k", [P, G, BC, LAGS], at=ctx)
        gates = sb("gates", [P, BC, LAGS], at=ctx)
        coef = sb("coef", [P, 2, BC, BW], at=ctx)
        v_tok = sb("v_tok", [P, NB, D], at=ctx)
        z_act = sb("z_act", [P, 2, CH], at=ctx)
        out_sq = sb("out_sq", [P, CH], at=ctx)
        o_buf = sb("o_buf", [P, 2, CH], at=ctx)
        bank_qv, bank_kz = banks[0], banks[1]
        bank_tqv, bank_tk = banks[2], banks[3]
        bank_out, bank_rq = banks2
        scores = pair[:, :].rearrange("p (b n) -> p b n", b=BC)[:, :, 0:BW]

        tables_in = sem("tables_in", ctx)
        cleared = sem("cleared", ctx)
        proj_done = {n: sem(f"proj_done_{n}", ctx) for n in "qkvz"}
        silu_done = {n: sem(f"silu_done_{n}", ctx) for n in "qkv"}
        tap_done = {n: sem(f"tap_done_{n}", ctx) for n in "qkv"}
        conv_done = {n: sem(f"conv_done_{n}", ctx) for n in "qkv"}
        rope_done = {n: sem(f"rope_done_{n}", ctx) for n in "qk"}
        swap_in = {n: [sem(f"swap_in_{n}{i}", ctx) for i in range(2)] for n in "qk"}
        turned_qk = sem("turned_qk", ctx)
        turned_v = sem("turned_v", ctx)
        norms_done = sem("norms_done", ctx)
        v_tok_done = sem("v_tok_done", ctx)
        floor_done = sem("floor_done", ctx)
        root_done = sem("root_done", ctx)
        rnorm_done = sem("rnorm_done", ctx)
        rq_picked = sem("rq_picked", ctx)
        scores_done = sem("scores_done", ctx)
        gates_done = sem("gates_done", ctx)
        gated = sem("gated", ctx)
        coef_done = sem("coef_done", ctx)
        out_done = sem("out_done", ctx)
        out_sq_done = sem("out_sq_done", ctx)
        z_done = sem("z_done", ctx)
        o_done = sem("o_done", ctx)
        sq_added = sem("sq_added", ctx)
        o_stored = [sem(f"o_stored{i}", ctx) for i in range(2)]
        block = ctx.enter_context(nc.Block())

        def back(h, g, k):
            h2, g2 = (h, g - k) if g >= k else (h - 1, g - k + G)
            if isinstance(h2, int) and not 0 <= h2 < H:
                return None
            return h2, g2

        def schedule(eng, step):
            for h in (0, 1):
                for g in range(G):
                    step(h, g)
            with eng.Fori(2, H - 1) as h:
                for g in range(G):
                    step(h, g)
            for g in range(G):
                step(H - 1, g)
            for g in range(3):
                step(H, g)

        def is_last(h):
            return isinstance(h, int) and h >= H - 1

        def cols(g):
            return slice(g * CH, (g + 1) * CH)

        @block.sync
        def _(sp):
            sp.dma_start(cos[:, :], env["rope_cos"]).then_inc(tables_in, 16)
            sp.dma_start(sin[:, :], env["rope_sin"]).then_inc(tables_in, 16)

            def load_weights(n, h):
                wait(sp, wlo_done[n], h)
                sp.dma_start(raw[n][:, :, :], w_slice(n, h)).then_inc(raw_in[n], 16)

            def step(h, g):
                c = h * G + g
                if not is_last(h):
                    if g == 0:
                        for n in "qkv":
                            load_weights(n, h + 1)
                    if g == 2:
                        load_weights("z", h + 1)
                if not (isinstance(h, int) and h >= H):
                    for n in "qk":
                        wait(sp, conv_done[n], 3 * c + 3)
                        wait(sp, rope_done[n], 3 * (c - 1))
                        for to, frm in ((0, HALF), (HALF, 0)):
                            sp.dma_start(swapped[n][to:to + HALF, g % 2, :], y[n][frm:frm + HALF, g % 2, :]
                                         ).then_inc(swap_in[n][g % 2], 16)
                if at := back(h, g, 3):
                    h3, g3 = at
                    wait(sp, o_done, c - 2)
                    sp.dma_start(o_scratch[bass.ds(h3 * D, D), cols(g3)], o_buf[:, g3 % 2, :]
                                 ).then_inc(o_stored[g3 % 2], 16)

            schedule(sp, step)
            for i in range(2):
                sp.wait_ge(o_stored[i], 16 * NC // 2)

        @block.gpsimd
        def _(pool):
            for n in "qkv":
                nc.gpsimd.memset(u[n][:, 0, 0:HALO], 0.0).then_inc(cleared, 1)
            nc.gpsimd.memset(rot["q"][:, S:S + LAGS], 0.0).then_inc(cleared, 1)
            nc.gpsimd.memset(rq_x[:, NB, :], 0.0).then_inc(cleared, 1)

            def split_lo(n, h):
                wait(pool, whi_done[n], h + 1)
                nc.gpsimd.tensor_tensor(w_lo[n][:, :, :], raw[n][:, :, :], w_hi[n][:, :, :].bitcast(fp32),
                                        ALU.subtract).then_inc(wlo_done[n], 1)

            def step(h, g):
                c = h * G + g
                if at := back(h, g, 1):
                    h1, g1 = at
                    blocks = slice(g1 * BC, (g1 + 1) * BC)
                    wait(pool, floor_done, c)
                    nc.gpsimd.tensor_tensor(rnorm[:, g1 % 2, :], norms[:, g1 % 2, :],
                                            neg_half[:, 0:2 * BC], ALU.pow).then_inc(root_done, 1)
                    wait(pool, root_done, c)
                    wait(pool, rq_picked, c - 3)
                    nc.gpsimd.tensor_tensor(
                        rq_x[:, blocks, :], rnorm[:, g1 % 2, 0:BC][:, :, None].broadcast_to([P, BC, LAGS]),
                        period[:, None, :].broadcast_to([P, BC, LAGS]), ALU.mult)
                    wait(pool, gates_done, c - 3)
                    nc.gpsimd.tensor_tensor(
                        gate_k[:, g1, :, :], gate0[:, blocks, bass.ds(h1 * LAGS, LAGS)],
                        rnorm[:, g1 % 2, BC:2 * BC][:, :, None].broadcast_to([P, BC, LAGS]),
                        ALU.mult).then_inc(rnorm_done, 1)
                if g == 1 and back(h, g, 0) and not (isinstance(h, int) and h == 0):
                    split_lo("z", h)
                if g == 3 and not is_last(h):
                    for n in "qkv":
                        split_lo(n, h + 1)

            schedule(pool, step)

        @block.scalar
        def _(act):
            act.wait_ge(cleared, 5)

            def split_hi(n, h, c):
                wait(act, raw_in[n], 16 * (h + 1))
                wait(act, proj_done[n], c + 1)
                nc.scalar.activation(w_hi[n][:, :, :], raw[n][:, :, :], ACT.Copy).then_inc(whi_done[n], 1)

            def silu_and_tap(n, bank, h, g, c):
                wait(act, proj_done[n], c + 1)
                wait(act, conv_done[n], 3 * (c - 1))
                nc.scalar.activation(u[n][:, g % 2, HALO:], bank[:, :], ACT.Silu).then_inc(silu_done[n], 1)
                wait(act, conv_done[n], 3 * c)
                wait(act, silu_done[n], 2 * c + 1)
                if n == "v":
                    wait(act, turned_v, c - 1)
                else:
                    wait(act, rope_done[n], 3 * (c - 1))
                    wait(act, turned_qk, c - 1)
                if g < G - 1:
                    nc.scalar.activation(u[n][:, (g + 1) % 2, 0:HALO], bank[:, CH - HALO:CH], ACT.Silu
                                         ).then_inc(silu_done[n], 1)
                else:
                    nc.scalar.activation(u[n][:, 0, 0:HALO], rot["q"][:, S:S + HALO], ACT.Copy
                                         ).then_inc(silu_done[n], 1)
                nc.scalar.activation(y[n][:, g % 2, :], u[n][:, g % 2, 0:CH], ACT.Copy,
                                     scale=cw[n][:, bass.ds(h * TAPS, 1)]).then_inc(tap_done[n], 1)

            def step(h, g):
                c = h * G + g
                front = back(h, g, 0)
                if at := back(h, g, 1):
                    g1 = at[1]
                    wait(act, turned_qk, c)
                    wait(act, rnorm_done, c - 2)
                    for i, bank in enumerate((bank_tqv, bank_tk)):
                        for b in range(BC):
                            block_of = bank[:, b * P:(b + 1) * P]
                            last = nc.scalar.activation(block_of, block_of, ACT.Square,
                                                        accum_out=norms[:, g1 % 2, i * BC + b:i * BC + b + 1])
                    last.then_inc(norms_done, 1)
                if front:
                    silu_and_tap("q", bank_qv, h, g, c)
                if front:
                    silu_and_tap("k", bank_kz, h, g, c)
                if at := back(h, g, 1):
                    g1 = at[1]
                    wait(act, turned_v, c)
                    wait(act, out_done, c - 3)
                    nc.scalar.activation(v_tok[:, g1 * BC:(g1 + 1) * BC, :],
                                         bank_tqv[:, :].rearrange("p (b d) -> p b d", b=BC),
                                         ACT.Copy).then_inc(v_tok_done, 1)
                if g == 3 and not is_last(h):
                    split_hi("q", h + 1, c)
                if front:
                    silu_and_tap("v", bank_qv, h, g, c)
                if g == 3 and not is_last(h):
                    split_hi("k", h + 1, c)
                    split_hi("v", h + 1, c)
                if back(h, g, 3):
                    wait(act, out_done, c - 2)
                    wait(act, sq_added, c - 3)
                    nc.scalar.activation(out_sq[:, :], bank_out[:, :], ACT.Square).then_inc(out_sq_done, 1)
                if at := back(h, g, 2):
                    g2 = at[1]
                    wait(act, proj_done["z"], c - 1)
                    wait(act, o_done, c - 3)
                    nc.scalar.activation(z_act[:, g2 % 2, :], bank_kz[:, :], ACT.Silu).then_inc(z_done, 1)
                if g == 1 and front and not (isinstance(h, int) and h == 0):
                    split_hi("z", h, c - 2)

            schedule(act, step)

        @block.vector
        def _(dve):
            dve.wait_ge(tables_in, 32)

            def conv_tap(n, i, h, g, c):
                if i == 1:
                    wait(dve, tap_done[n], c + 1)
                else:
                    wait(dve, conv_done[n], 3 * c + i - 1)
                nc.vector.scalar_tensor_tensor(
                    y[n][:, g % 2, :], u[n][:, g % 2, i:i + CH], cw[n][:, bass.ds(h * TAPS + i, 1)],
                    y[n][:, g % 2, :], ALU.mult, ALU.add).then_inc(conv_done[n], 1)

            def rope(n, i, g, c):
                to, sw = rot[n][:, cols(g)], swapped[n][:, g % 2, :]
                if i == 0:
                    wait(dve, conv_done[n], 3 * c + 3)
                    wait(dve, scores_done, c - 3)
                    op = nc.vector.tensor_tensor(to, y[n][:, g % 2, :], cos[:, cols(g)], ALU.mult)
                elif i == 1:
                    wait(dve, swap_in[n][g % 2], 32 * (c // 2 + 1) if isinstance(c, int) else
                         c * 16 + (32 if g % 2 == 0 else 16))
                    op = nc.vector.tensor_tensor(sw, sw, sin[:, cols(g)], ALU.mult)
                else:
                    wait(dve, rope_done[n], 3 * c + 2)
                    op = nc.vector.tensor_tensor(to, to, sw, ALU.add)
                op.then_inc(rope_done[n], 1)

            def step(h, g):
                c = h * G + g
                if at := back(h, g, 1):
                    g1 = at[1]
                    wait(dve, norms_done, c)
                    nc.vector.tensor_scalar(norms[:, g1 % 2, :], norms[:, g1 % 2, :], NORM_FLOOR, None, ALU.max
                                            ).then_inc(floor_done, 1)
                if back(h, g, 0):
                    for i in (1, 2, 3):
                        conv_tap("q", i, h, g, c)
                        conv_tap("k", i, h, g, c)
                    conv_tap("v", 1, h, g, c)
                    rope("q", 0, g, c)
                    conv_tap("v", 2, h, g, c)
                    rope("k", 0, g, c)
                    conv_tap("v", 3, h, g, c)
                    for i in (1, 2):
                        rope("q", i, g, c)
                        rope("k", i, g, c)
                at2, at3 = back(h, g, 2), back(h, g, 3)
                if at2:
                    h2, g2 = at2
                    w = coef[:, g2 % 2, :, :]
                    wait(dve, rq_picked, c - 1)
                    nc.vector.tensor_tensor(gates[:, :, :],
                                            bank_rq[:, 0:BC * LAGS].rearrange("p (b r) -> p b r", b=BC),
                                            gate_k[:, g2, :, :], ALU.mult).then_inc(gates_done, 1)
                    wait(dve, scores_done, c - 1)
                    wait(dve, out_done, c - 2)
                    wait(dve, gates_done, c - 1)
                    nc.vector.tensor_tensor(
                        w.rearrange("p b (a r) -> p b a r", r=LAGS),
                        scores.rearrange("p b (a r) -> p b a r", r=LAGS),
                        gates[:, :, None, :].broadcast_to([P, BC, BW // LAGS, LAGS]),
                        ALU.mult).then_inc(gated, 1)
                if at3:
                    h3, g3 = at3
                    wait(dve, out_sq_done, c - 2)
                    wait(dve, z_done, c - 2)
                    wait(dve, o_stored[g3 % 2], 16 * ((c - 3) // 2) if isinstance(c, int) else
                         8 * (c - 3) - (8 if g3 % 2 else 0))
                    nc.vector.scalar_tensor_tensor(o_buf[:, g3 % 2, :], bank_out[:, :],
                                                   nw_sb[:, bass.ds(h3, 1)], z_act[:, g3 % 2, :],
                                                   ALU.mult, ALU.mult).then_inc(o_done, 1)
                if at2:
                    wait(dve, gated, c - 1)
                    nc.vector.tensor_tensor(w, w, band[:, None, :].broadcast_to([P, BC, BW]), ALU.mult
                                            ).then_inc(coef_done, 1)
                if at3:
                    nc.vector.tensor_tensor(sq_sum[:, cols(g3)], sq_sum[:, cols(g3)], out_sq[:, :], ALU.add
                                            ).then_inc(sq_added, 1)

            schedule(dve, step)

        @block.tensor
        def _(pe):
            pe.wait_ge(cleared, 5)

            def project(n, bank, h, g, c):
                wait(pe, wlo_done[n], h + 1)
                terms = [(w, part, t) for w, part in ((w_hi, x_hi), (w_lo, x_hi), (w_hi, x_lo))
                         for t in range(KT)]
                for i, (w, part, t) in enumerate(terms):
                    last = nc.tensor.matmul(bank[:, :], w[n][:, t, :], part[:, t, cols(g)],
                                            start=(i == 0), stop=(i == len(terms) - 1))
                last.then_inc(proj_done[n], 1)

            def step(h, g):
                c = h * G + g
                front = back(h, g, 0)
                at1, at2, at3 = (back(h, g, k) for k in (1, 2, 3))
                if at1:
                    g1 = at1[1]
                    wait(pe, v_tok_done, c - 1)
                    wait(pe, norms_done, c - 1)
                    for n, bank in (("q", bank_tqv), ("k", bank_tk)):
                        wait(pe, conv_done[n], 3 * c)
                        for b in range(BC):
                            last = nc.tensor.transpose(bank[:, b * P:(b + 1) * P],
                                                       y[n][:, g1 % 2, b * P:(b + 1) * P], ident)
                    last.then_inc(turned_qk, 1)
                if front:
                    wait(pe, silu_done["v"], 2 * c)
                    project("q", bank_qv, h, g, c)
                if front:
                    wait(pe, z_done, c - 2)
                    project("k", bank_kz, h, g, c)
                if at1:
                    g1 = at1[1]
                    wait(pe, norms_done, c)
                    wait(pe, conv_done["v"], 3 * c)
                    for b in range(BC):
                        last = nc.tensor.transpose(bank_tqv[:, b * P:(b + 1) * P],
                                                   y["v"][:, g1 % 2, b * P:(b + 1) * P], ident)
                    last.then_inc(turned_v, 1)
                if front:
                    wait(pe, silu_done["q"], 2 * c + 2)
                    project("v", bank_qv, h, g, c)
                if at3:
                    g3 = at3[1]
                    wait(pe, coef_done, c - 2)
                    wait(pe, v_tok_done, c - 2)
                    wait(pe, o_done, c - 3)
                    if g3 > 0:
                        nc.tensor.matmul(bank_out[:, 0:LAGS], v_tok[:, g3 * BC - 1, :],
                                         coef[:, (g3 - 1) % 2, BC - 1, P:BW], start=True, stop=False,
                                         skip_group_check=True)
                    for b in range(BC):
                        width = BW if b < BC - 1 else P
                        last = nc.tensor.matmul(bank_out[:, b * P:b * P + width], v_tok[:, g3 * BC + b, :],
                                                coef[:, g3 % 2, b, 0:width], start=(b == 0 and g3 == 0),
                                                stop=(b == BC - 1), skip_group_check=True)
                    last.then_inc(out_done, 1)
                if at2:
                    if front:
                        wait(pe, silu_done["k"], 2 * c + 2)
                    else:
                        wait(pe, z_done, c - 2)
                    project("z", bank_kz, at2[0], at2[1], c - 2)
                    g2 = at2[1]
                    ahead = 1 if g2 < G - 1 else 0
                    wait(pe, rnorm_done, c - 1 + ahead)
                    wait(pe, gates_done, c - 2)
                    own = rq_x[:, g2 * BC:(g2 + 1) * BC, :].rearrange("p b r -> p (b r)")
                    after = rq_x[:, g2 * BC + 1:(g2 + 1) * BC + 1, :].rearrange("p b r -> p (b r)")
                    nc.tensor.matmul(bank_rq[:, 0:BC * LAGS], sel_own, own, start=True, stop=False)
                    nc.tensor.matmul(bank_rq[:, 0:BC * LAGS], sel_next, after, start=False, stop=True
                                     ).then_inc(rq_picked, 1)
                    wait(pe, rope_done["q"], 3 * (c - 1 + ahead))
                    wait(pe, rope_done["k"], 3 * (c - 1))
                    wait(pe, gated, c - 2)
                    for b in range(BC):
                        at = (g2 * BC + b) * P
                        last = nc.tensor.matmul(scores[:, b, :], rot["k"][:, at:at + P], rot["q"][:, at:at + BW],
                                                start=True, stop=True)
                    last.then_inc(scores_done, 1)

            schedule(pe, step)


def ffn_and_output(nc, env):
    (fp32, f32r, ALU, ACT, P, S, HID, KT, H, D, HD, FT, CH, G, BC, NB, RMS_EPS, sb, sem, wait) = (
        env[n] for n in ("fp32", "f32r", "ALU", "ACT", "P", "S", "HID", "KT", "H", "D", "HD", "FT", "CH", "G",
                         "BC", "NB", "RMS_EPS", "sb", "sem", "wait"))
    (neg_half, x_hi, x_lo, sq_sum, us_sb, banks, pair, banks2, o_scratch) = (
        env[n] for n in ("neg_half", "x_hi", "x_lo", "sq_sum", "us_sb", "banks", "pair", "banks2",
                         "o_scratch"))
    with ExitStack() as late:
        g_scratch = nc.dram_tensor("g_scratch", [S, HID], fp32).ap().rearrange("(b p) d -> p b d", p=P)
        with ExitStack() as ctx:
            WG = 2
            up_raw = sb("up_raw", [P, 2, KT, WG * P], at=ctx)
            down_raw = sb("down_raw", [P, 2, WG, HID], at=ctx)
            up_sign = sb("up_sign", [P, KT, FT * P], f32r, at=ctx)
            down_sign = sb("down_sign", [P, FT, HID], f32r, at=ctx)
            scale_row = sb("scale_row", [P, HID], at=ctx)
            out_scale = sb("out_scale", [P, 1], at=ctx)
            g_buf = sb("g_buf", [P, BC, HID], at=ctx)
            relu = sb("relu", [P, 2, CH], at=ctx)
            hid_hi = sb("hid_hi", [P, 2, CH], f32r, at=ctx)
            hid_lo = sb("hid_lo", [P, 2, CH], f32r, at=ctx)
            up_in = [sem(f"up_in{i}", ctx) for i in range(2)]
            down_in = [sem(f"down_in{i}", ctx) for i in range(2)]
            scale_in = sem("scale_in", ctx)
            scaled = sem("scaled", ctx)
            up_signed = sem("up_signed", ctx)
            down_signed = sem("down_signed", ctx)
            up_done = sem("up_done", ctx)
            relu_done = sem("relu_done", ctx)
            hid_hi_done = sem("hid_hi_done", ctx)
            hid_lo_done = sem("hid_lo_done", ctx)
            down_done = sem("down_done", ctx)
            acc_read = sem("acc_read", ctx)
            g_done = sem("g_done", ctx)
            g_stored = sem("g_stored", ctx)
            up_banks = banks2
            acc = [banks[0], banks[1], banks[2], banks[3]]
            block = ctx.enter_context(nc.Block())

            @block.sync
            def _(sp):
                sp.dma_start(scale_row[:, :], env["down_scale"].partition_broadcast(P)).then_inc(scale_in, 16)
                sp.dma_start(out_scale[:, :], env["output_scale"].partition_broadcast(P)).then_inc(scale_in, 16)
                for i in range(FT // WG):
                    wait(sp, up_signed, i - 1)
                    sp.dma_start(up_raw[:, i % 2, :, :],
                                 env["up_t"].rearrange("(t p) n -> p t n", p=P)[:, :, i * WG * P:(i + 1) * WG * P]
                                 ).then_inc(up_in[i % 2], 16)
                    wait(sp, down_signed, i - 1)
                    sp.dma_start(down_raw[:, i % 2, :, :],
                                 env["down_t"].rearrange("(j p) n -> p j n", p=P)[:, i * WG:(i + 1) * WG, :]
                                 ).then_inc(down_in[i % 2], 16)

                def store(n):
                    wait(sp, g_done, (n + 1) * BC)
                    sp.dma_start(g_scratch[:, bass.ds(n * BC, BC), :], g_buf[:, :, :]).then_inc(g_stored, 16)

                store(0)
                with sp.Fori(1, G) as n:
                    store(n)
                sp.wait_ge(g_stored, 16 * G)

            @block.scalar
            def _(act):
                def signs(i):
                    act.wait_ge(up_in[i % 2], 16 * (i // 2 + 1))
                    nc.scalar.activation(up_sign[:, :, i * WG * P:(i + 1) * WG * P], up_raw[:, i % 2, :, :],
                                         ACT.Sign).then_inc(up_signed, 1)
                    act.wait_ge(down_in[i % 2], 16 * (i // 2 + 1))
                    nc.scalar.activation(down_sign[:, i * WG:(i + 1) * WG, :], down_raw[:, i % 2, :, :],
                                         ACT.Sign).then_inc(down_signed, 1)

                def hidden(n, j):
                    i = n * FT + j
                    wait(act, up_done, i + 1)
                    wait(act, hid_lo_done, i - 1)
                    nc.scalar.activation(relu[:, j % 2, :], up_banks[j % 2][:, :], ACT.Relu,
                                         scale=us_sb[:, j:j + 1]).then_inc(relu_done, 1)
                    wait(act, relu_done, i + 1)
                    wait(act, down_done, i - 1)
                    nc.scalar.activation(hid_hi[:, j % 2, :], relu[:, j % 2, :], ACT.Copy
                                         ).then_inc(hid_hi_done, 1)

                def finish(n):
                    for b in range(BC):
                        wait(act, acc_read, n * BC + b + 1)
                        nc.scalar.activation(g_buf[:, b, :], g_buf[:, b, :], ACT.Silu).then_inc(g_done, 1)

                signs(0)
                for j in range(FT):
                    if j % WG == 0 and j // WG + 1 < FT // WG:
                        signs(j // WG + 1)
                    hidden(0, j)
                finish(0)
                with act.Fori(1, G) as n:
                    for j in range(FT):
                        hidden(n, j)
                    finish(n)

            @block.vector
            def _(dve):
                dve.wait_ge(scale_in, 32)
                nc.vector.tensor_scalar(scale_row[:, :], scale_row[:, :], out_scale[:, 0:1], None, ALU.mult
                                        ).then_inc(scaled, 1)
                dve.wait_ge(scaled, 1)

                def chunk(n):
                    for j in range(FT):
                        i = n * FT + j
                        wait(dve, hid_hi_done, i + 1)
                        wait(dve, down_done, i - 1)
                        nc.vector.tensor_tensor(hid_lo[:, j % 2, :], relu[:, j % 2, :],
                                                hid_hi[:, j % 2, :].bitcast(fp32), ALU.subtract
                                                ).then_inc(hid_lo_done, 1)
                    wait(dve, down_done, (n + 1) * FT)
                    wait(dve, g_stored, 16 * n)
                    for b in range(BC):
                        nc.vector.tensor_tensor(g_buf[:, b, :], acc[b][:, :], scale_row[:, :], ALU.mult
                                                ).then_inc(acc_read, 1)

                chunk(0)
                with dve.Fori(1, G) as n:
                    chunk(n)

            @block.tensor
            def _(pe):
                def up(n, j):
                    i = n * FT + j
                    if isinstance(n, int) and n == 0:
                        wait(pe, up_signed, j // WG + 1)
                    wait(pe, relu_done, i - 1)
                    for k in range(2 * KT):
                        part, t = (x_hi, x_lo)[k // KT], k % KT
                        last = nc.tensor.matmul(up_banks[j % 2][:, :], up_sign[:, t, j * P:(j + 1) * P],
                                                part[:, t, bass.ds(n * CH, CH)],
                                                start=(k == 0), stop=(k == 2 * KT - 1))
                    last.then_inc(up_done, 1)

                def down(n, j):
                    i = n * FT + j
                    if isinstance(n, int) and n == 0:
                        wait(pe, down_signed, j // WG + 1)
                    wait(pe, hid_lo_done, i + 1)
                    for b in range(BC):
                        if j == 0:
                            wait(pe, acc_read, (n - 1) * BC + b + 1)
                        for part in (hid_hi, hid_lo):
                            last = nc.tensor.matmul(acc[b][:, :], part[:, j % 2, b * P:(b + 1) * P],
                                                    down_sign[:, j, :], start=(j == 0 and part is hid_hi),
                                                    stop=(j == FT - 1 and part is hid_lo))
                    last.then_inc(down_done, 1)

                def chunk(n):
                    up(n, 0)
                    for j in range(FT):
                        if j + 1 < FT:
                            up(n, j + 1)
                        down(n, j)

                chunk(0)
                with pe.Fori(1, G) as n:
                    chunk(n)

        with ExitStack() as ctx:
            WR = 4
            wo_raw = sb("wo_raw", [P, 2, HID], at=ctx)
            wo_hi = sb("wo_hi", [P, H, HID], f32r, at=ctx)
            wo_lo = sb("wo_lo", [P, H, HID], f32r, at=ctx)
            o_raw = sb("o_raw", [P, WR, CH], at=ctx)
            o_hi = sb("o_hi", [P, 2, CH], f32r, at=ctx)
            o_lo = sb("o_lo", [P, 2, CH], f32r, at=ctx)
            ones = sb("ones", [P, 2], at=ctx)
            mean_sq = sb("mean_sq", [P, NB], at=ctx)
            rms = sb("rms", [P, NB], at=ctx)
            x_res = sb("x_res", [P, BC, HID], at=ctx)
            g_res = sb("g_res", [P, BC, HID], at=ctx)
            y_out = sb("y_out", [P, BC, HID], at=ctx)
            wo_in = [sem(f"wo_in{i}", ctx) for i in range(2)]
            o_in = [sem(f"o_in{i}", ctx) for i in range(WR)]
            wo_hi_done = sem("wo_hi_done", ctx)
            wo_lo_done = sem("wo_lo_done", ctx)
            o_hi_done = sem("o_hi_done", ctx)
            o_lo_done = sem("o_lo_done", ctx)
            ones_set = sem("ones_set", ctx)
            sq_total = sem("sq_total", ctx)
            mean_done = sem("mean_done", ctx)
            rms_done = sem("rms_done", ctx)
            proj_used = sem("proj_used", ctx)
            x_res_in = sem("x_res_in", ctx)
            g_res_in = sem("g_res_in", ctx)
            gated_out = sem("gated_out", ctx)
            y_done = sem("y_done", ctx)
            y_stored = sem("y_stored", ctx)
            acc = banks
            bank_sq = banks2[0]
            x_view = env["x"].rearrange("(b p) d -> p b d", p=P)
            out_view = env["out"].rearrange("(b p) d -> p b d", p=P)
            block = ctx.enter_context(nc.Block())

            @block.sync
            def _(sp):
                def chunk(n):
                    for h in range(H):
                        i = n * H + h
                        if isinstance(n, int) and n == 0:
                            wait(sp, wo_lo_done, h - 1)
                            sp.dma_start(wo_raw[:, h % 2, :], env["wout"][h * D:(h + 1) * D, :]
                                         ).then_inc(wo_in[h % 2], 16)
                        wait(sp, o_lo_done, i - WR + 1)
                        sp.dma_start(o_raw[:, h % WR, :], o_scratch[h * D:(h + 1) * D, bass.ds(n * CH, CH)]
                                     ).then_inc(o_in[h % WR], 16)
                        if h == 1:
                            wait(sp, y_done, n * BC)
                            sp.dma_start(x_res[:, :, :], x_view[:, bass.ds(n * BC, BC), :]
                                         ).then_inc(x_res_in, 16)
                            sp.dma_start(g_res[:, :, :], g_scratch[:, bass.ds(n * BC, BC), :]
                                         ).then_inc(g_res_in, 16)
                    wait(sp, y_done, (n + 1) * BC)
                    sp.dma_start(out_view[:, bass.ds(n * BC, BC), :], y_out[:, :, :]).then_inc(y_stored, 16)

                chunk(0)
                with sp.Fori(1, G) as n:
                    chunk(n)
                sp.wait_ge(y_stored, 16 * G)

            @block.gpsimd
            def _(pool):
                nc.gpsimd.memset(ones[:, :], 1.0).then_inc(ones_set, 1)
                pool.wait_ge(mean_done, 1)
                nc.gpsimd.tensor_tensor(rms[:, :], mean_sq[:, :], neg_half[:, 0:NB], ALU.pow
                                        ).then_inc(rms_done, 1)

            @block.scalar
            def _(act):
                def chunk(n):
                    for h in range(H):
                        i = n * H + h
                        if isinstance(n, int) and n == 0:
                            act.wait_ge(wo_in[h % 2], 16 * (h // 2 + 1))
                            nc.scalar.activation(wo_hi[:, h, :], wo_raw[:, h % 2, :], ACT.Copy
                                                 ).then_inc(wo_hi_done, 1)
                        wait(act, o_in[h % WR], 16 * (n * (H // WR) + h // WR + 1))
                        wait(act, proj_used, i - 1)
                        nc.scalar.activation(o_hi[:, h % 2, :], o_raw[:, h % WR, :], ACT.Copy
                                             ).then_inc(o_hi_done, 1)

                chunk(0)
                with act.Fori(1, G) as n:
                    chunk(n)

            @block.vector
            def _(dve):
                dve.wait_ge(sq_total, 1)
                nc.vector.tensor_scalar(mean_sq[:, :], bank_sq[:, 0:2 * NB].rearrange("p (b r) -> p b r", r=2)[:, :, 0],
                                        1.0 / HD, RMS_EPS, ALU.mult, ALU.add).then_inc(mean_done, 1)

                def chunk(n):
                    for h in range(H):
                        i = n * H + h
                        if isinstance(n, int) and n == 0:
                            dve.wait_ge(wo_hi_done, h + 1)
                            nc.vector.tensor_tensor(wo_lo[:, h, :], wo_raw[:, h % 2, :],
                                                    wo_hi[:, h, :].bitcast(fp32), ALU.subtract
                                                    ).then_inc(wo_lo_done, 1)
                        wait(dve, o_hi_done, i + 1)
                        wait(dve, proj_used, i - 1)
                        nc.vector.tensor_tensor(o_lo[:, h % 2, :], o_raw[:, h % WR, :],
                                                o_hi[:, h % 2, :].bitcast(fp32), ALU.subtract
                                                ).then_inc(o_lo_done, 1)
                    wait(dve, proj_used, (n + 1) * H)
                    wait(dve, rms_done, 1)
                    wait(dve, g_res_in, 16 * (n + 1))
                    wait(dve, y_stored, 16 * n)
                    for b in range(BC):
                        at = n * BC + b
                        nc.vector.scalar_tensor_tensor(
                            y_out[:, b, :], acc[b][:, :], rms[:, bass.ds(at, 1)], g_res[:, b, :], ALU.mult, ALU.mult).then_inc(gated_out, 1)
                    wait(dve, x_res_in, 16 * (n + 1))
                    for b in range(BC):
                        wait(dve, gated_out, n * BC + b + 1)
                        nc.vector.tensor_tensor(y_out[:, b, :], y_out[:, b, :], x_res[:, b, :], ALU.add
                                                ).then_inc(y_done, 1)

                chunk(0)
                with dve.Fori(1, G) as n:
                    chunk(n)

            @block.tensor
            def _(pe):
                pe.wait_ge(ones_set, 1)
                for b in range(NB):
                    last = nc.tensor.matmul(bank_sq[:, 2 * b:2 * b + 2], sq_sum[:, b * P:(b + 1) * P],
                                            ones[:, :], start=True, stop=True)
                last.then_inc(sq_total, 1)

                def chunk(n):
                    for h in range(H):
                        i = n * H + h
                        if isinstance(n, int) and n == 0:
                            wait(pe, wo_lo_done, h + 1)
                        wait(pe, o_lo_done, i + 1)
                        for b in range(BC):
                            if h == 0:
                                wait(pe, gated_out, (n - 1) * BC + b + 1)
                            for k, (part, w) in enumerate(((o_hi, wo_hi), (o_lo, wo_hi), (o_hi, wo_lo))):
                                last = nc.tensor.matmul(acc[b][:, :], part[:, h % 2, b * P:(b + 1) * P],
                                                        w[:, h, :], start=(h == 0 and k == 0),
                                                        stop=(h == H - 1 and k == 2))
                        last.then_inc(proj_used, 1)

                chunk(0)
                with pe.Fori(1, G) as n:
                    chunk(n)


def shape_constants(seq, head, lags):
    import numpy as np

    p = np.arange(128)
    own = p[:, None] - p[None, :]
    after = own + 128
    band = np.arange(128 + lags)[None, :] - p[:, None]
    masks = np.concatenate([
        np.eye(128),
        (own >= 0) & (own < lags),
        (after >= 0) & (after < lags),
        (band >= 0) & (band < lags),
        (p[:, None] % lags) == np.arange(lags)[None, :],
    ], axis=1).astype(np.float32)
    inv = np.float32(1.0) / np.power(np.float32(1e6), np.arange(0, head, 2, dtype=np.float32) / np.float32(head),
                                     dtype=np.float32)
    angle = (inv[:, None] * np.arange(seq, dtype=np.float32)[None, :]).astype(np.float64)
    cos = np.concatenate([np.cos(angle), np.cos(angle)], 0).astype(np.float32)
    sin = np.concatenate([-np.sin(angle), np.sin(angle)], 0).astype(np.float32)
    return masks, cos, sin


def kernel(**inputs):
    import numpy as np
    import concourse.bacc as bacc
    from concourse import mybir
    from concourse.bass_utils import run_bass_kernel_spmd

    given = {n.replace("L0_attn_", "").replace("L0_ffn_", ""): np.asarray(a) for n, a in inputs.items()}
    _, seq, hid = given["x"].shape
    heads = given["Wa"].shape[1]

    def by_tile(a):
        a = a.reshape(a.shape[0] // 128, 128, -1)
        return np.ascontiguousarray(a.transpose(1, 0, 2).reshape(128, -1))

    masks, cos, sin = shape_constants(seq, given["Wq"].shape[1] // heads, 4)
    arrays = {
        "x": given["x"].reshape(seq, hid),
        "wq": given["Wq"], "wk": given["Wk"], "wv": given["Wv"], "wz": given["Wz"],
        "wa": given["Wa"], "wb": given["Wb"],
        "conv_q": by_tile(given["conv_q_w"]), "conv_k": by_tile(given["conv_k_w"]),
        "conv_v": by_tile(given["conv_v_w"]), "norm_w": by_tile(given["norm_w"]),
        "wout": given["Wout"],
        "up_t": np.ascontiguousarray(given["up_weight"].T),
        "down_t": np.ascontiguousarray(given["down_weight"].T),
        "up_scale": by_tile(given["up_scale"]),
        "down_scale": given["down_scale"], "output_scale": given["output_scale"],
        "masks": masks, "rope_cos": cos, "rope_sin": sin,
    }
    nc = bacc.Bacc("TRN2", target_bir_lowering=False, num_devices=1)
    args, feed = {}, {}
    for name, a in arrays.items():
        a = np.ascontiguousarray(a)
        feed[f"in_{name}"] = a
        args[name] = nc.dram_tensor(f"in_{name}", a.shape, mybir.dt.from_np(a.dtype), kind="ExternalInput").ap()
    args["out"] = nc.dram_tensor("out_y", (seq, hid), mybir.dt.float32, kind="ExternalOutput").ap()
    gated_recurrent_block_kernel(nc, **args)
    result = run_bass_kernel_spmd(nc, [feed], core_ids=[0])
    return result.results[0]["out_y"].reshape(1, seq, hid)
```

```python
import concourse.bass as bass
from concourse import mybir
from contextlib import ExitStack


def gated_recurrent_block_kernel(
    nc: bass.Bass,
    x: bass.AP,
    wq: bass.AP,
    wk: bass.AP,
    wv: bass.AP,
    wz: bass.AP,
    wa: bass.AP,
    wb: bass.AP,
    conv_q: bass.AP,
    conv_k: bass.AP,
    conv_v: bass.AP,
    norm_w: bass.AP,
    wout: bass.AP,
    up_t: bass.AP,
    down_t: bass.AP,
    up_scale: bass.AP,
    down_scale: bass.AP,
    output_scale: bass.AP,
    masks: bass.AP,
    rope_cos: bass.AP,
    rope_sin: bass.AP,
    out: bass.AP,
):
    fp32 = mybir.dt.float32
    f32r = mybir.dt.float32r
    ALU = mybir.AluOpType
    ACT = mybir.ActivationFunctionType

    P = 128
    S, HID = x.shape
    KT = HID // P
    HD = wq.shape[1]
    D = P
    H = HD // D
    FH = up_t.shape[1]
    FT = FH // P
    CH = 512
    G = S // CH
    BC = CH // P
    NB = S // P
    LAGS = 4
    HALO = LAGS - 1
    TAPS = 4
    BW = P + LAGS
    AB = 2 * H
    LN_EPS, RMS_EPS, NORM_FLOOR = 1e-5, 1e-6, 1e-24
    SCALE = float(D) ** -0.5

    C_ID, C_SEL, C_HALO, C_BAND, C_PER = 0, P, 2 * P, 3 * P, 3 * P + BW

    o_scratch = nc.dram_tensor("o_scratch", [HD, S], fp32).ap()

    def wait(eng, sem, count):
        if isinstance(count, int) and count <= 0:
            return
        eng.wait_ge(sem, count)

    top = ExitStack()
    with top:
        def sb(name, shape, dt=fp32, at=top):
            return at.enter_context(nc.sbuf_tensor(name, shape, dt))

        def sem(name, at=top):
            return at.enter_context(nc.semaphore(name))

        const = sb("const", [P, masks.shape[1]])
        neg_half = sb("neg_half", [P, 2 * NB])
        x_hi = sb("x_hi", [P, KT, S], f32r)
        x_lo = sb("x_lo", [P, KT, S], f32r)
        sq_sum = sb("sq_sum", [P, S])
        nw_sb = sb("nw_sb", [P, H])
        us_sb = sb("us_sb", [P, FT])
        WG = 2
        up_raw = sb("up_raw", [P, 2, KT, WG * P])
        down_raw = sb("down_raw", [P, 2, WG, HID])
        up_in = [sem(f"up_in{i}") for i in range(2)]
        down_in = [sem(f"down_in{i}") for i in range(2)]

        def load_ffn_weights(sp, i):
            sp.dma_start(up_raw[:, i % 2, :, :],
                         up_t.rearrange("(t p) n -> p t n", p=P)[:, :, i * WG * P:(i + 1) * WG * P]
                         ).then_inc(up_in[i % 2], 16)
            sp.dma_start(down_raw[:, i % 2, :, :],
                         down_t.rearrange("(j p) n -> p j n", p=P)[:, i * WG:(i + 1) * WG, :]
                         ).then_inc(down_in[i % 2], 16)

        ident = const[:, C_ID:C_ID + P]
        sel_own = const[:, C_SEL:C_SEL + P]
        sel_next = const[:, C_HALO:C_HALO + P]
        band = const[:, C_BAND:C_BAND + BW]
        period = const[:, C_PER:C_PER + LAGS]

        banks = [top.enter_context(nc.psum_tensor(f"bank{i}", [P, 512], fp32)) for i in range(4)]
        pair = top.enter_context(nc.psum_tensor("bank45", [P, 1024], fp32))
        banks2 = [top.enter_context(nc.psum_tensor(f"bank{i}", [P, 512], fp32)) for i in (6, 7)]

        att = ExitStack()
        with att:
            cw = {n: sb(f"cw_{n}", [P, H * TAPS], at=att) for n in "qkv"}
            gate0 = sb("gate0", [P, NB, H * LAGS], at=att)
            raw = {n: sb(f"raw_{n}", [P, KT, D], at=att) for n in "qkvz"}
            w_hi = {n: sb(f"whi_{n}", [P, KT, D], f32r, at=att) for n in "qkvz"}
            w_lo = {n: sb(f"wlo_{n}", [P, KT, D], f32r, at=att) for n in "qkvz"}
            w_dram = {"q": wq, "k": wk, "v": wv, "z": wz}
            raw_in = {n: sem(f"raw_in_{n}", att) for n in "qkvz"}
            whi_done = {n: sem(f"whi_done_{n}", att) for n in "qkvz"}
            wlo_done = {n: sem(f"wlo_done_{n}", att) for n in "qkvz"}

            def w_slice(n, h):
                return w_dram[n].rearrange("(t p) n -> p t n", p=P)[:, :, bass.ds(h * D, D)]

            attention(nc, locals())

        ffn_and_output(nc, locals())


def attention(nc, env):
    (fp32, f32r, ALU, ACT, P, S, HID, KT, H, D, CH, G, BC, NB, LAGS, HALO, TAPS, BW, AB, SCALE, LN_EPS,
     NORM_FLOOR, sb, sem, wait) = (
        env[n] for n in ("fp32", "f32r", "ALU", "ACT", "P", "S", "HID", "KT", "H", "D", "CH", "G", "BC", "NB",
                         "LAGS", "HALO", "TAPS", "BW", "AB", "SCALE", "LN_EPS", "NORM_FLOOR", "sb", "sem",
                         "wait"))
    (const, neg_half, x_hi, x_lo, sq_sum, ident, sel_own, sel_next, band, period, banks, pair, banks2, cw, gate0,
     raw, w_hi, w_lo, raw_in, whi_done, wlo_done, w_slice, nw_sb, us_sb, o_scratch, up_raw, down_raw) = (
        env[n] for n in ("const", "neg_half", "x_hi", "x_lo", "sq_sum", "ident", "sel_own", "sel_next", "band",
                         "period", "banks", "pair", "banks2", "cw", "gate0", "raw", "w_hi", "w_lo", "raw_in",
                         "whi_done", "wlo_done", "w_slice", "nw_sb", "us_sb", "o_scratch", "up_raw",
                         "down_raw"))
    NC = H * G
    HALF = D // 2
    with ExitStack() as ctx:
        cos = sb("cos", [P, S], at=ctx)
        sin = sb("sin", [P, S], at=ctx)
        u = {n: sb(f"u_{n}", [P, 2, CH + HALO], at=ctx) for n in "qkv"}
        y = {n: sb(f"y_{n}", [P, 2, CH], at=ctx) for n in "qkv"}
        swapped = {n: sb(f"swapped_{n}", [P, 2, CH], at=ctx) for n in "qk"}
        rot = {"q": sb("rot_q", [P, S + LAGS], at=ctx), "k": sb("rot_k", [P, S], at=ctx)}
        norms = sb("norms", [P, 2, 2 * BC], at=ctx)
        rnorm = sb("rnorm", [P, 2, 2 * BC], at=ctx)
        rq_x = sb("rq_x", [P, (NB + 1), LAGS], at=ctx)
        gate_k = sb("gate_k", [P, G, BC, LAGS], at=ctx)
        gates = sb("gates", [P, BC, LAGS], at=ctx)
        coef = sb("coef", [P, 2, BC, BW], at=ctx)
        v_tok = sb("v_tok", [P, NB, D], at=ctx)
        z_act = sb("z_act", [P, 2, CH], at=ctx)
        out_sq = sb("out_sq", [P, CH], at=ctx)
        o_buf = sb("o_buf", [P, 2, CH], at=ctx)
        bank_qv, bank_kz = banks[0], banks[1]
        bank_tqv, bank_tk = banks[2], banks[3]
        bank_out, bank_rq = banks2
        scores = pair[:, :].rearrange("p (b n) -> p b n", b=BC)[:, :, 0:BW]

        stats = sb("stats", [P, NB, 6], at=ctx)
        mean_var = sb("mean_var", [P, NB, 2], at=ctx)
        rstd = sb("rstd", [P, NB], at=ctx)

        def flat(t, dims):
            return t if dims == 2 else t.rearrange("p a b -> p (a b)" if dims == 3 else "p a b c -> p (a b c)")

        homes = (flat(up_raw[:, :, :, :], 4), flat(down_raw[:, :, :, :], 4), flat(v_tok[:, :, :], 3),
                 rot["k"][:, :])
        xt = [home.rearrange("p (b d) -> p b d", b=BC) for home in homes]
        ab_raw, ab_hi, ab_lo = raw["z"], w_hi["z"], w_lo["z"]
        ab_t = rot["q"][0:AB, 0:S]
        ab = out_sq[:, :].rearrange("p (b n) -> p b n", b=NB)
        bx = flat(v_tok[:, :, :], 3)[:, 0:(NB + 1) * H * LAGS].rearrange(
            "p (b h r) -> p b h r", b=NB + 1, h=H)
        ab_banks = (pair[:, 0:CH], pair[:, CH:2 * CH], banks2[0][:, :], banks2[1][:, :])
        bank_ab, pick_banks = pair[:, 0:CH], (pair[:, CH:2 * CH], banks2[0][:, :])
        HALF_NB = NB // 2

        const_in = sem("const_in", ctx)
        x_in = [sem(f"x_in{g}", ctx) for g in range(G)]
        small_in = sem("small_in", ctx)
        ab_zeroed = sem("ab_zeroed", ctx)
        root_set = sem("root_set", ctx)
        ab_in = sem("ab_in", ctx)
        stats_done = sem("stats_done", ctx)
        moments = sem("moments", ctx)
        var_eps = sem("var_eps", ctx)
        rstd_done = sem("rstd_done", ctx)
        normed = sem("normed", ctx)
        turned_x = sem("turned_x", ctx)
        hi_done = sem("hi_done", ctx)
        lo_done = sem("lo_done", ctx)
        abw_hi = sem("abw_hi", ctx)
        abw_lo = sem("abw_lo", ctx)
        ab_proj = sem("ab_proj", ctx)
        abt_done = sem("abt_done", ctx)
        ab_turned = sem("ab_turned", ctx)
        ab_done = sem("ab_done", ctx)
        bx_done = sem("bx_done", ctx)
        picked = sem("picked", ctx)
        prod_done = sem("prod_done", ctx)
        tanh_done = sem("tanh_done", ctx)
        gate_done = sem("gate_done", ctx)

        tables_in = sem("tables_in", ctx)
        cleared = sem("cleared", ctx)
        proj_done = {n: sem(f"proj_done_{n}", ctx) for n in "qkvz"}
        silu_done = {n: sem(f"silu_done_{n}", ctx) for n in "qkv"}
        tap_done = {n: sem(f"tap_done_{n}", ctx) for n in "qkv"}
        conv_done = {n: sem(f"conv_done_{n}", ctx) for n in "qkv"}
        rope_done = {n: sem(f"rope_done_{n}", ctx) for n in "qk"}
        swap_in = {n: [sem(f"swap_in_{n}{i}", ctx) for i in range(2)] for n in "qk"}
        turned_qk = sem("turned_qk", ctx)
        turned_v = sem("turned_v", ctx)
        norms_done = sem("norms_done", ctx)
        v_tok_done = sem("v_tok_done", ctx)
        floor_done = sem("floor_done", ctx)
        root_done = sem("root_done", ctx)
        rnorm_done = sem("rnorm_done", ctx)
        rq_picked = sem("rq_picked", ctx)
        scores_done = sem("scores_done", ctx)
        gates_done = sem("gates_done", ctx)
        gated = sem("gated", ctx)
        coef_done = sem("coef_done", ctx)
        out_done = sem("out_done", ctx)
        out_sq_done = sem("out_sq_done", ctx)
        z_done = sem("z_done", ctx)
        o_done = sem("o_done", ctx)
        sq_added = sem("sq_added", ctx)
        o_stored = [sem(f"o_stored{i}", ctx) for i in range(2)]
        block = ctx.enter_context(nc.Block())

        def back(h, g, k):
            h2, g2 = (h, g - k) if g >= k else (h - 1, g - k + G)
            if isinstance(h2, int) and not 0 <= h2 < H:
                return None
            return h2, g2

        def schedule(eng, step):
            for h in (0, 1):
                for g in range(G):
                    step(h, g)
            with eng.Fori(2, H - 1) as h:
                for g in range(G):
                    step(h, g)
            for g in range(G):
                step(H - 1, g)
            for g in range(3):
                step(H, g)

        def is_start(h, g):
            return isinstance(h, int) and h == 0 and g == 0

        def is_last(h):
            return isinstance(h, int) and h >= H - 1

        def cols(g):
            return slice(g * CH, (g + 1) * CH)

        @block.sync
        def _(sp):
            def load_x(g):
                sp.dma_start(xt[g], env["x"].rearrange("(b p) d -> p b d", p=P)[:, g * BC:(g + 1) * BC, :]
                             ).then_inc(x_in[g], 16)

            load_x(0)
            sp.dma_start(const[:, :], env["masks"]).then_inc(const_in, 16)
            load_x(1)
            wait(sp, ab_zeroed, 1)
            sp.dma_start(ab_raw[:, :, 0:H], env["wa"].rearrange("(t p) n -> p t n", p=P)).then_inc(ab_in, 16)
            sp.dma_start(ab_raw[:, :, H:AB], env["wb"].rearrange("(t p) n -> p t n", p=P)).then_inc(ab_in, 16)
            load_x(2)
            load_x(3)
            for n in "qkv":
                sp.dma_start(raw[n][:, :, :], w_slice(n, 0)).then_inc(raw_in[n], 16)
            for n in "qkv":
                sp.dma_start(cw[n][:, :], env[f"conv_{n}"]).then_inc(small_in, 16)
            sp.dma_start(nw_sb[:, :], env["norm_w"]).then_inc(small_in, 16)
            sp.dma_start(us_sb[:, :], env["up_scale"]).then_inc(small_in, 16)
            sp.dma_start(cos[:, :], env["rope_cos"]).then_inc(tables_in, 16)
            sp.dma_start(sin[:, :], env["rope_sin"]).then_inc(tables_in, 16)
            wait(sp, abw_lo, 1)
            sp.dma_start(raw["z"][:, :, :], w_slice("z", 0)).then_inc(raw_in["z"], 16)
            wait(sp, turned_x, 2 * BC)

            def load_weights(n, h):
                wait(sp, wlo_done[n], h)
                sp.dma_start(raw[n][:, :, :], w_slice(n, h)).then_inc(raw_in[n], 16)

            def step(h, g):
                c = h * G + g
                if not is_last(h):
                    if g == 0:
                        for n in "qkv":
                            load_weights(n, h + 1)
                    if g == 2:
                        load_weights("z", h + 1)
                if not (isinstance(h, int) and h >= H):
                    for n in "qk":
                        wait(sp, conv_done[n], 3 * c + 3)
                        wait(sp, rope_done[n], 3 * (c - 1))
                        for to, frm in ((0, HALF), (HALF, 0)):
                            sp.dma_start(swapped[n][to:to + HALF, g % 2, :], y[n][frm:frm + HALF, g % 2, :]
                                         ).then_inc(swap_in[n][g % 2], 16)
                if at := back(h, g, 3):
                    h3, g3 = at
                    wait(sp, o_done, c - 2)
                    sp.dma_start(o_scratch[bass.ds(h3 * D, D), cols(g3)], o_buf[:, g3 % 2, :]
                                 ).then_inc(o_stored[g3 % 2], 16)

            for i in range(2):
                env["load_ffn_weights"](sp, i)
            schedule(sp, step)
            for i in range(2):
                sp.wait_ge(o_stored[i], 16 * NC // 2)

        @block.gpsimd
        def _(pool):
            nc.gpsimd.memset(ab_raw[:, :, :], 0.0).then_inc(ab_zeroed, 1)
            nc.gpsimd.memset(neg_half[:, :], -0.5).then_inc(root_set, 1)
            for n in "qkv":
                nc.gpsimd.memset(u[n][:, 0, 0:HALO], 0.0).then_inc(cleared, 1)
            nc.gpsimd.memset(rot["q"][:, S:S + LAGS], 0.0).then_inc(cleared, 1)
            nc.gpsimd.memset(rq_x[:, NB, :], 0.0).then_inc(cleared, 1)
            nc.gpsimd.memset(sq_sum[:, :], 0.0).then_inc(cleared, 1)
            pool.wait_ge(root_set, 1)
            for g in range(G):
                part = slice(g * BC, (g + 1) * BC)
                pool.wait_ge(moments, (g + 1) * BC)
                nc.gpsimd.tensor_scalar(rstd[:, part], mean_var[:, part, 1], LN_EPS, None, ALU.add
                                        ).then_inc(var_eps, 1)
                pool.wait_ge(var_eps, g + 1)
                nc.gpsimd.tensor_tensor(rstd[:, part], rstd[:, part], neg_half[:, part], ALU.pow
                                        ).then_inc(rstd_done, 1)

            def split_lo(n, h):
                wait(pool, whi_done[n], h + 1)
                nc.gpsimd.tensor_tensor(w_lo[n][:, :, :], raw[n][:, :, :], w_hi[n][:, :, :].bitcast(fp32),
                                        ALU.subtract).then_inc(wlo_done[n], 1)

            for n in "qkvz":
                split_lo(n, 0)
            pool.wait_ge(const_in, 16)
            pool.wait_ge(gate_done, 2)

            def step(h, g):
                c = h * G + g
                if at := back(h, g, 1):
                    h1, g1 = at
                    blocks = slice(g1 * BC, (g1 + 1) * BC)
                    wait(pool, floor_done, c)
                    nc.gpsimd.tensor_tensor(rnorm[:, g1 % 2, :], norms[:, g1 % 2, :],
                                            neg_half[:, 0:2 * BC], ALU.pow).then_inc(root_done, 1)
                    wait(pool, root_done, c)
                    wait(pool, rq_picked, c - 3)
                    nc.gpsimd.tensor_tensor(
                        rq_x[:, blocks, :], rnorm[:, g1 % 2, 0:BC][:, :, None].broadcast_to([P, BC, LAGS]),
                        period[:, None, :].broadcast_to([P, BC, LAGS]), ALU.mult)
                    wait(pool, gates_done, c - 3)
                    nc.gpsimd.tensor_tensor(
                        gate_k[:, g1, :, :], gate0[:, blocks, bass.ds(h1 * LAGS, LAGS)],
                        rnorm[:, g1 % 2, BC:2 * BC][:, :, None].broadcast_to([P, BC, LAGS]),
                        ALU.mult).then_inc(rnorm_done, 1)
                if g == 1 and back(h, g, 0) and not (isinstance(h, int) and h == 0):
                    split_lo("z", h)
                if g == 3 and not is_last(h):
                    for n in "qkv":
                        split_lo(n, h + 1)

            schedule(pool, step)

        @block.scalar
        def _(act):
            act.wait_ge(ab_in, 32)
            nc.scalar.activation(ab_hi[:, :, :], ab_raw[:, :, :], ACT.Copy).then_inc(abw_hi, 1)
            for b in range(NB):
                act.wait_ge(turned_x, b + 1)
                nc.scalar.activation(x_hi[:, :, b * P:(b + 1) * P],
                                     banks[b % 4][:, :].rearrange("p (t n) -> p t n", t=KT),
                                     ACT.Copy).then_inc(hi_done, 1)
                if b >= NB - 3:
                    n = "qkv"[b - NB + 3]
                    act.wait_ge(raw_in[n], 16)
                    nc.scalar.activation(w_hi[n][:, :, :], raw[n][:, :, :], ACT.Copy).then_inc(whi_done[n], 1)
            for g in range(G):
                act.wait_ge(ab_proj, g + 1)
                nc.scalar.activation(ab_t[:, g * CH:(g + 1) * CH], ab_banks[g][0:AB, :], ACT.Copy
                                     ).then_inc(abt_done, 1)
            act.wait_ge(raw_in["z"], 16)
            nc.scalar.activation(w_hi["z"][:, :, :], raw["z"][:, :, :], ACT.Copy).then_inc(whi_done["z"], 1)
            act.wait_ge(small_in, 16 * 5)
            act.wait_ge(cleared, 6)

            def split_hi(n, h, c):
                wait(act, raw_in[n], 16 * (h + 1))
                wait(act, proj_done[n], c + 1)
                nc.scalar.activation(w_hi[n][:, :, :], raw[n][:, :, :], ACT.Copy).then_inc(whi_done[n], 1)

            def silu_and_tap(n, bank, h, g, c):
                wait(act, proj_done[n], c + 1)
                wait(act, conv_done[n], 3 * (c - 1))
                nc.scalar.activation(u[n][:, g % 2, HALO:], bank[:, :], ACT.Silu).then_inc(silu_done[n], 1)
                wait(act, conv_done[n], 3 * c)
                wait(act, silu_done[n], 2 * c + 1)
                if n == "v":
                    wait(act, turned_v, c - 1)
                else:
                    wait(act, rope_done[n], 3 * (c - 1))
                    wait(act, turned_qk, c - 1)
                if g < G - 1:
                    nc.scalar.activation(u[n][:, (g + 1) % 2, 0:HALO], bank[:, CH - HALO:CH], ACT.Silu
                                         ).then_inc(silu_done[n], 1)
                else:
                    nc.scalar.activation(u[n][:, 0, 0:HALO], rot["q"][:, S:S + HALO], ACT.Copy
                                         ).then_inc(silu_done[n], 1)
                nc.scalar.activation(y[n][:, g % 2, :], u[n][:, g % 2, 0:CH], ACT.Copy,
                                     scale=cw[n][:, bass.ds(h * TAPS, 1)]).then_inc(tap_done[n], 1)

            def step(h, g):
                c = h * G + g
                front = back(h, g, 0)
                if at := back(h, g, 1):
                    g1 = at[1]
                    wait(act, turned_qk, c)
                    wait(act, rnorm_done, c - 2)
                    for i, bank in enumerate((bank_tqv, bank_tk)):
                        for b in range(BC):
                            block_of = bank[:, b * P:(b + 1) * P]
                            last = nc.scalar.activation(block_of, block_of, ACT.Square,
                                                        accum_out=norms[:, g1 % 2, i * BC + b:i * BC + b + 1])
                    last.then_inc(norms_done, 1)
                if front:
                    silu_and_tap("q", bank_qv, h, g, c)
                if front:
                    silu_and_tap("k", bank_kz, h, g, c)
                if at := back(h, g, 1):
                    g1 = at[1]
                    wait(act, turned_v, c)
                    wait(act, out_done, c - 3)
                    nc.scalar.activation(v_tok[:, g1 * BC:(g1 + 1) * BC, :],
                                         bank_tqv[:, :].rearrange("p (b d) -> p b d", b=BC),
                                         ACT.Copy).then_inc(v_tok_done, 1)
                if g == 3 and not is_last(h):
                    split_hi("q", h + 1, c)
                if front:
                    silu_and_tap("v", bank_qv, h, g, c)
                if g == 3 and not is_last(h):
                    split_hi("k", h + 1, c)
                    split_hi("v", h + 1, c)
                if back(h, g, 3):
                    wait(act, out_done, c - 2)
                    wait(act, sq_added, c - 3)
                    nc.scalar.activation(out_sq[:, :], bank_out[:, :], ACT.Square).then_inc(out_sq_done, 1)
                if is_start(h, g):
                    for i in range(2):
                        part = gate0[:, i * HALF_NB:(i + 1) * HALF_NB, :]
                        act.wait_ge(prod_done, i + 1)
                        nc.scalar.activation(part, part, ACT.Tanh, scale=0.5).then_inc(tanh_done, 1)
                if at := back(h, g, 2):
                    g2 = at[1]
                    wait(act, proj_done["z"], c - 1)
                    wait(act, o_done, c - 3)
                    nc.scalar.activation(z_act[:, g2 % 2, :], bank_kz[:, :], ACT.Silu).then_inc(z_done, 1)
                if g == 1 and front and not (isinstance(h, int) and h == 0):
                    split_hi("z", h, c - 2)

            schedule(act, step)

        @block.vector
        def _(dve):
            def moments_of(g):
                dve.wait_ge(x_in[g], 16)
                for b in range(g * BC, (g + 1) * BC):
                    nc.vector.bn_stats(stats[:, b, :], xt[g][:, b % BC, :]).then_inc(stats_done, 1)
                for b in range(g * BC, (g + 1) * BC):
                    dve.wait_ge(stats_done, b + 1)
                    nc.vector.bn_aggr(mean_var[:, b, :], stats[:, b, :]).then_inc(moments, 1)

            def normalize(b):
                part = xt[b // BC][:, b % BC, :]
                dve.wait_ge(rstd_done, b // BC + 1)
                nc.vector.tensor_scalar(part, part, mean_var[:, b, 0:1], rstd[:, b:b + 1],
                                        ALU.subtract, ALU.mult).then_inc(normed, 1)

            moments_of(0)
            moments_of(1)
            for b in range(BC):
                normalize(b)
            for b in range(NB):
                if b % BC == 0 and b // BC + 2 < G:
                    moments_of(b // BC + 2)
                if b == BC:
                    dve.wait_ge(abw_hi, 1)
                    nc.vector.tensor_tensor(ab_lo[:, :, :], ab_raw[:, :, :], ab_hi[:, :, :].bitcast(fp32),
                                            ALU.subtract).then_inc(abw_lo, 1)
                if b + BC < NB:
                    normalize(b + BC)
                dve.wait_ge(hi_done, b + 1)
                nc.vector.tensor_tensor(
                    x_lo[:, :, b * P:(b + 1) * P], banks[b % 4][:, :].rearrange("p (t n) -> p t n", t=KT),
                    x_hi[:, :, b * P:(b + 1) * P].bitcast(fp32), ALU.subtract).then_inc(lo_done, 1)
            dve.wait_ge(ab_turned, 1)
            nc.vector.tensor_copy(ab, bank_ab.rearrange("p (b n) -> p b n", b=NB)).then_inc(ab_done, 1)
            nc.vector.memset(bx[:, NB, :, :], 0.0).then_inc(bx_done, 1)
            dve.wait_ge(ab_done, 1)
            dve.wait_ge(const_in, 16)
            for r in range(LAGS):
                nc.vector.tensor_scalar(bx[:, 0:NB, :, r], ab[:, :, H:AB], period[:, r:r + 1], None, ALU.mult
                                        ).then_inc(bx_done, 1)
            dve.wait_ge(tables_in, 32)

            def conv_tap(n, i, h, g, c):
                if i == 1:
                    wait(dve, tap_done[n], c + 1)
                else:
                    wait(dve, conv_done[n], 3 * c + i - 1)
                nc.vector.scalar_tensor_tensor(
                    y[n][:, g % 2, :], u[n][:, g % 2, i:i + CH], cw[n][:, bass.ds(h * TAPS + i, 1)],
                    y[n][:, g % 2, :], ALU.mult, ALU.add).then_inc(conv_done[n], 1)

            def rope(n, i, g, c):
                to, sw = rot[n][:, cols(g)], swapped[n][:, g % 2, :]
                if i == 0:
                    wait(dve, conv_done[n], 3 * c + 3)
                    wait(dve, scores_done, c - 3)
                    op = nc.vector.tensor_tensor(to, y[n][:, g % 2, :], cos[:, cols(g)], ALU.mult)
                elif i == 1:
                    wait(dve, swap_in[n][g % 2], 32 * (c // 2 + 1) if isinstance(c, int) else
                         c * 16 + (32 if g % 2 == 0 else 16))
                    op = nc.vector.tensor_tensor(sw, sw, sin[:, cols(g)], ALU.mult)
                else:
                    wait(dve, rope_done[n], 3 * c + 2)
                    op = nc.vector.tensor_tensor(to, to, sw, ALU.add)
                op.then_inc(rope_done[n], 1)

            def step(h, g):
                c = h * G + g
                if at := back(h, g, 1):
                    g1 = at[1]
                    wait(dve, norms_done, c)
                    nc.vector.tensor_scalar(norms[:, g1 % 2, :], norms[:, g1 % 2, :], NORM_FLOOR, None, ALU.max
                                            ).then_inc(floor_done, 1)
                if back(h, g, 0):
                    for i in (1, 2, 3):
                        conv_tap("q", i, h, g, c)
                        conv_tap("k", i, h, g, c)
                    conv_tap("v", 1, h, g, c)
                    rope("q", 0, g, c)
                    conv_tap("v", 2, h, g, c)
                    rope("k", 0, g, c)
                    conv_tap("v", 3, h, g, c)
                    for i in (1, 2):
                        rope("q", i, g, c)
                        rope("k", i, g, c)
                if is_start(h, g):
                    for i in range(2):
                        blocks = slice(i * HALF_NB, (i + 1) * HALF_NB)
                        dve.wait_ge(picked, i + 1)
                        nc.vector.tensor_tensor(
                            gate0[:, blocks, :].rearrange("p b (h r) -> p b h r", h=H),
                            pick_banks[i].rearrange("p (b h r) -> p b h r", b=HALF_NB, h=H),
                            ab[:, blocks, 0:H][:, :, :, None].broadcast_to([P, HALF_NB, H, LAGS]),
                            ALU.mult).then_inc(prod_done, 1)
                    for i in range(2):
                        part = gate0[:, i * HALF_NB:(i + 1) * HALF_NB, :]
                        dve.wait_ge(tanh_done, i + 1)
                        nc.vector.tensor_scalar(part, part, 1.0, 0.5 * SCALE, ALU.add, ALU.mult
                                                ).then_inc(gate_done, 1)
                at2, at3 = back(h, g, 2), back(h, g, 3)
                if at2:
                    h2, g2 = at2
                    w = coef[:, g2 % 2, :, :]
                    wait(dve, rq_picked, c - 1)
                    nc.vector.tensor_tensor(gates[:, :, :],
                                            bank_rq[:, 0:BC * LAGS].rearrange("p (b r) -> p b r", b=BC),
                                            gate_k[:, g2, :, :], ALU.mult).then_inc(gates_done, 1)
                    wait(dve, scores_done, c - 1)
                    wait(dve, out_done, c - 2)
                    wait(dve, gates_done, c - 1)
                    nc.vector.tensor_tensor(
                        w.rearrange("p b (a r) -> p b a r", r=LAGS),
                        scores.rearrange("p b (a r) -> p b a r", r=LAGS),
                        gates[:, :, None, :].broadcast_to([P, BC, BW // LAGS, LAGS]),
                        ALU.mult).then_inc(gated, 1)
                if at3:
                    h3, g3 = at3
                    wait(dve, out_sq_done, c - 2)
                    wait(dve, z_done, c - 2)
                    wait(dve, o_stored[g3 % 2], 16 * ((c - 3) // 2) if isinstance(c, int) else
                         8 * (c - 3) - (8 if g3 % 2 else 0))
                    nc.vector.scalar_tensor_tensor(o_buf[:, g3 % 2, :], bank_out[:, :],
                                                   nw_sb[:, bass.ds(h3, 1)], z_act[:, g3 % 2, :],
                                                   ALU.mult, ALU.mult).then_inc(o_done, 1)
                if at2:
                    wait(dve, gated, c - 1)
                    nc.vector.tensor_tensor(w, w, band[:, None, :].broadcast_to([P, BC, BW]), ALU.mult
                                            ).then_inc(coef_done, 1)
                if at3:
                    nc.vector.tensor_tensor(sq_sum[:, cols(g3)], sq_sum[:, cols(g3)], out_sq[:, :], ALU.add
                                            ).then_inc(sq_added, 1)

            schedule(dve, step)

        @block.tensor
        def _(pe):
            def turn_x(g):
                for b in range(g * BC, (g + 1) * BC):
                    pe.wait_ge(normed, b + 1)
                    wait(pe, lo_done, b - 3)
                    for t in range(KT):
                        last = nc.tensor.transpose(banks[b % 4][:, t * P:(t + 1) * P],
                                                   xt[g][:, b % BC, t * P:(t + 1) * P], ident)
                    last.then_inc(turned_x, 1)

            def project_ab(g):
                pe.wait_ge(lo_done, (g + 1) * BC)
                terms = [(w, part, t) for w, part in ((ab_hi, x_hi), (ab_lo, x_hi), (ab_hi, x_lo))
                         for t in range(KT)]
                for i, (w, part, t) in enumerate(terms):
                    last = nc.tensor.matmul(ab_banks[g], w[:, t, :], part[:, t, cols(g)],
                                            start=(i == 0), stop=(i == len(terms) - 1))
                last.then_inc(ab_proj, 1)

            pe.wait_ge(const_in, 16)
            turn_x(0)
            turn_x(1)
            pe.wait_ge(abw_lo, 1)
            project_ab(0)
            turn_x(2)
            project_ab(1)
            turn_x(3)
            project_ab(2)
            project_ab(3)
            pe.wait_ge(cleared, 6)

            def project(n, bank, h, g, c):
                wait(pe, wlo_done[n], h + 1)
                terms = [(w, part, t) for w, part in ((w_hi, x_hi), (w_lo, x_hi), (w_hi, x_lo))
                         for t in range(KT)]
                for i, (w, part, t) in enumerate(terms):
                    last = nc.tensor.matmul(bank[:, :], w[n][:, t, :], part[:, t, cols(g)],
                                            start=(i == 0), stop=(i == len(terms) - 1))
                last.then_inc(proj_done[n], 1)

            def step(h, g):
                c = h * G + g
                front = back(h, g, 0)
                at1, at2, at3 = (back(h, g, k) for k in (1, 2, 3))
                if at1:
                    g1 = at1[1]
                    wait(pe, v_tok_done, c - 1)
                    wait(pe, norms_done, c - 1)
                    for n, bank in (("q", bank_tqv), ("k", bank_tk)):
                        wait(pe, conv_done[n], 3 * c)
                        for b in range(BC):
                            last = nc.tensor.transpose(bank[:, b * P:(b + 1) * P],
                                                       y[n][:, g1 % 2, b * P:(b + 1) * P], ident)
                    last.then_inc(turned_qk, 1)
                if front:
                    wait(pe, silu_done["v"], 2 * c)
                    project("q", bank_qv, h, g, c)
                if is_start(h, g):
                    pe.wait_ge(abt_done, G)
                    for b in range(NB):
                        last = nc.tensor.transpose(bank_ab[:, b * AB:(b + 1) * AB], ab_t[:, b * P:(b + 1) * P],
                                                   ident[0:AB, 0:AB])
                    last.then_inc(ab_turned, 1)
                if front:
                    wait(pe, z_done, c - 2)
                    project("k", bank_kz, h, g, c)
                if is_start(h, g):
                    pe.wait_ge(bx_done, LAGS + 1)
                    for i in range(2):
                        own = bx[:, i * HALF_NB:(i + 1) * HALF_NB, :, :].rearrange("p b h r -> p (b h r)")
                        after = bx[:, i * HALF_NB + 1:(i + 1) * HALF_NB + 1, :, :].rearrange(
                            "p b h r -> p (b h r)")
                        nc.tensor.matmul(pick_banks[i], sel_own, own, start=True, stop=False)
                        nc.tensor.matmul(pick_banks[i], sel_next, after, start=False, stop=True
                                         ).then_inc(picked, 1)
                if at1:
                    g1 = at1[1]
                    wait(pe, norms_done, c)
                    wait(pe, conv_done["v"], 3 * c)
                    for b in range(BC):
                        last = nc.tensor.transpose(bank_tqv[:, b * P:(b + 1) * P],
                                                   y["v"][:, g1 % 2, b * P:(b + 1) * P], ident)
                    last.then_inc(turned_v, 1)
                if front:
                    wait(pe, silu_done["q"], 2 * c + 2)
                    project("v", bank_qv, h, g, c)
                if at3:
                    g3 = at3[1]
                    wait(pe, coef_done, c - 2)
                    wait(pe, v_tok_done, c - 2)
                    wait(pe, o_done, c - 3)
                    if g3 > 0:
                        nc.tensor.matmul(bank_out[:, 0:LAGS], v_tok[:, g3 * BC - 1, :],
                                         coef[:, (g3 - 1) % 2, BC - 1, P:BW], start=True, stop=False,
                                         skip_group_check=True)
                    for b in range(BC):
                        width = BW if b < BC - 1 else P
                        last = nc.tensor.matmul(bank_out[:, b * P:b * P + width], v_tok[:, g3 * BC + b, :],
                                                coef[:, g3 % 2, b, 0:width], start=(b == 0 and g3 == 0),
                                                stop=(b == BC - 1), skip_group_check=True)
                    last.then_inc(out_done, 1)
                if at2:
                    if front:
                        wait(pe, silu_done["k"], 2 * c + 2)
                    else:
                        wait(pe, z_done, c - 2)
                    project("z", bank_kz, at2[0], at2[1], c - 2)
                    g2 = at2[1]
                    ahead = 1 if g2 < G - 1 else 0
                    wait(pe, rnorm_done, c - 1 + ahead)
                    wait(pe, gates_done, c - 2)
                    own = rq_x[:, g2 * BC:(g2 + 1) * BC, :].rearrange("p b r -> p (b r)")
                    after = rq_x[:, g2 * BC + 1:(g2 + 1) * BC + 1, :].rearrange("p b r -> p (b r)")
                    nc.tensor.matmul(bank_rq[:, 0:BC * LAGS], sel_own, own, start=True, stop=False)
                    nc.tensor.matmul(bank_rq[:, 0:BC * LAGS], sel_next, after, start=False, stop=True
                                     ).then_inc(rq_picked, 1)
                    wait(pe, rope_done["q"], 3 * (c - 1 + ahead))
                    wait(pe, rope_done["k"], 3 * (c - 1))
                    wait(pe, gated, c - 2)
                    for b in range(BC):
                        at = (g2 * BC + b) * P
                        last = nc.tensor.matmul(scores[:, b, :], rot["k"][:, at:at + P], rot["q"][:, at:at + BW],
                                                start=True, stop=True)
                    last.then_inc(scores_done, 1)

            schedule(pe, step)


def ffn_and_output(nc, env):
    (fp32, f32r, ALU, ACT, P, S, HID, KT, H, D, HD, FT, CH, G, BC, NB, RMS_EPS, sb, sem, wait) = (
        env[n] for n in ("fp32", "f32r", "ALU", "ACT", "P", "S", "HID", "KT", "H", "D", "HD", "FT", "CH", "G",
                         "BC", "NB", "RMS_EPS", "sb", "sem", "wait"))
    (neg_half, x_hi, x_lo, sq_sum, us_sb, banks, banks2, o_scratch, WG, up_raw, down_raw, up_in,
     down_in, load_ffn_weights) = (
        env[n] for n in ("neg_half", "x_hi", "x_lo", "sq_sum", "us_sb", "banks", "banks2",
                         "o_scratch", "WG", "up_raw", "down_raw", "up_in", "down_in", "load_ffn_weights"))
    g_scratch = nc.dram_tensor("g_scratch", [S, HID], fp32).ap().rearrange("(b p) d -> p b d", p=P)
    x_view = env["x"].rearrange("(b p) d -> p b d", p=P)
    out_view = env["out"].rearrange("(b p) d -> p b d", p=P)
    WR = 4
    with ExitStack() as ctx:
        up_sign = sb("up_sign", [P, KT, FT * P], f32r, at=ctx)
        down_sign = sb("down_sign", [P, FT, HID], f32r, at=ctx)
        scale_row = sb("scale_row", [P, HID], at=ctx)
        out_scale = sb("out_scale", [P, 1], at=ctx)
        relu = sb("relu", [P, 2, CH], at=ctx)
        hid_hi = sb("hid_hi", [P, 2, CH], f32r, at=ctx)
        hid_lo = sb("hid_lo", [P, 2, CH], f32r, at=ctx)
        g_buf = sb("g_buf", [P, BC, HID], at=ctx)
        wo_raw = sb("wo_raw", [P, 2, HID], at=ctx)
        o_raw = sb("o_raw", [P, WR, CH], at=ctx)
        ones = sb("ones", [P, 2], at=ctx)
        mean_sq = sb("mean_sq", [P, NB], at=ctx)
        rms = sb("rms", [P, NB], at=ctx)
        wo_hi = x_hi[:, :, :].rearrange("p t (a n) -> p (t a) n", n=HID)
        wo_lo = x_lo[:, :, :].rearrange("p t (a n) -> p (t a) n", n=HID)
        o_hi, o_lo, y_out = hid_hi, hid_lo, g_buf
        x_res = up_raw[:, :, :, :].rearrange("p a t n -> p (a t n)").rearrange("p (b d) -> p b d", b=BC)
        g_res = down_raw[:, :, :, :].rearrange("p a t n -> p (a t n)").rearrange("p (b d) -> p b d", b=BC)
        acc = banks
        up_banks = banks2
        bank_sq = banks2[0]

        scale_in = sem("scale_in", ctx)
        scaled = sem("scaled", ctx)
        up_signed = sem("up_signed", ctx)
        down_signed = sem("down_signed", ctx)
        up_done = sem("up_done", ctx)
        relu_done = sem("relu_done", ctx)
        hid_hi_done = sem("hid_hi_done", ctx)
        hid_lo_done = sem("hid_lo_done", ctx)
        down_done = sem("down_done", ctx)
        acc_read = sem("acc_read", ctx)
        g_done = sem("g_done", ctx)
        g_stored = sem("g_stored", ctx)
        wo_in = [sem(f"wo_in{i}", ctx) for i in range(2)]
        o_in = [sem(f"o_in{i}", ctx) for i in range(WR)]
        wo_hi_done = sem("wo_hi_done", ctx)
        wo_lo_done = sem("wo_lo_done", ctx)
        o_hi_done = sem("o_hi_done", ctx)
        o_lo_done = sem("o_lo_done", ctx)
        ones_set = sem("ones_set", ctx)
        sq_total = sem("sq_total", ctx)
        mean_done = sem("mean_done", ctx)
        rms_done = sem("rms_done", ctx)
        proj_used = sem("proj_used", ctx)
        x_res_in = sem("x_res_in", ctx)
        g_res_in = sem("g_res_in", ctx)
        gated_out = sem("gated_out", ctx)
        y_done = sem("y_done", ctx)
        y_stored = sem("y_stored", ctx)
        block = ctx.enter_context(nc.Block())

        def is_first(n):
            return isinstance(n, int) and n == 0

        @block.sync
        def _(sp):
            def load_wout(h):
                sp.dma_start(wo_raw[:, h % 2, :], env["wout"][h * D:(h + 1) * D, :]).then_inc(wo_in[h % 2], 16)

            def load_o(n, h):
                sp.dma_start(o_raw[:, h % WR, :], o_scratch[h * D:(h + 1) * D, bass.ds(n * CH, CH)]
                             ).then_inc(o_in[h % WR], 16)

            def store_g(n):
                wait(sp, g_done, (n + 1) * BC)
                sp.dma_start(g_scratch[:, bass.ds(n * BC, BC), :], g_buf[:, :, :]).then_inc(g_stored, 16)

            def store_y(n):
                for b in range(BC):
                    wait(sp, y_done, n * BC + b + 1)
                    sp.dma_start(out_view[:, bass.ds(n * BC + b, 1), :], y_out[:, b:b + 1, :]
                                 ).then_inc(y_stored, 16)

            def out_chunk(n):
                for h in range(H):
                    if is_first(n) and h >= 2:
                        wait(sp, wo_lo_done, h - 1)
                        load_wout(h)
                    if not is_first(n) or h >= WR:
                        wait(sp, o_lo_done, n * H + h - WR + 1)
                        load_o(n, h)
                    if h == 10:
                        if is_first(n):
                            wait(sp, up_signed, FT // WG)
                            wait(sp, down_signed, FT // WG)
                            wait(sp, g_stored, 16 * G)
                        else:
                            store_y(n - 1)
                        sp.dma_start(x_res, x_view[:, bass.ds(n * BC, BC), :]).then_inc(x_res_in, 16)
                        sp.dma_start(g_res, g_scratch[:, bass.ds(n * BC, BC), :]).then_inc(g_res_in, 16)

            sp.dma_start(scale_row[:, :], env["down_scale"].partition_broadcast(P)).then_inc(scale_in, 16)
            sp.dma_start(out_scale[:, :], env["output_scale"].partition_broadcast(P)).then_inc(scale_in, 16)
            for i in range(2, FT // WG):
                wait(sp, up_signed, i - 1)
                wait(sp, down_signed, i - 1)
                load_ffn_weights(sp, i)
            load_wout(0)
            load_wout(1)
            for h in range(WR):
                load_o(0, h)
            store_g(0)
            with sp.Fori(1, G) as n:
                store_g(n)
            out_chunk(0)
            with sp.Fori(1, G) as n:
                out_chunk(n)
            store_y(G - 1)
            sp.wait_ge(y_stored, 16 * NB)

        @block.gpsimd
        def _(pool):
            nc.gpsimd.memset(ones[:, :], 1.0).then_inc(ones_set, 1)
            pool.wait_ge(mean_done, 1)
            nc.gpsimd.tensor_tensor(rms[:, :], mean_sq[:, :], neg_half[:, 0:NB], ALU.pow).then_inc(rms_done, 1)

        @block.scalar
        def _(act):
            def signs(i):
                act.wait_ge(up_in[i % 2], 16 * (i // 2 + 1))
                nc.scalar.activation(up_sign[:, :, i * WG * P:(i + 1) * WG * P], up_raw[:, i % 2, :, :],
                                     ACT.Sign).then_inc(up_signed, 1)
                act.wait_ge(down_in[i % 2], 16 * (i // 2 + 1))
                nc.scalar.activation(down_sign[:, i * WG:(i + 1) * WG, :], down_raw[:, i % 2, :, :],
                                     ACT.Sign).then_inc(down_signed, 1)

            def hidden(n, j):
                i = n * FT + j
                wait(act, up_done, i + 1)
                wait(act, hid_lo_done, i - 1)
                nc.scalar.activation(relu[:, j % 2, :], up_banks[j % 2][:, :], ACT.Relu,
                                     scale=us_sb[:, j:j + 1]).then_inc(relu_done, 1)
                wait(act, relu_done, i + 1)
                wait(act, down_done, i - 1)
                nc.scalar.activation(hid_hi[:, j % 2, :], relu[:, j % 2, :], ACT.Copy).then_inc(hid_hi_done, 1)

            def silu_g(n):
                for b in range(BC):
                    wait(act, acc_read, n * BC + b + 1)
                    nc.scalar.activation(g_buf[:, b, :], g_buf[:, b, :], ACT.Silu).then_inc(g_done, 1)

            def out_chunk(n):
                for h in range(H):
                    if is_first(n):
                        act.wait_ge(wo_in[h % 2], 16 * (h // 2 + 1))
                        act.wait_ge(up_done, G * FT)
                        nc.scalar.activation(wo_hi[:, h, :], wo_raw[:, h % 2, :], ACT.Copy
                                             ).then_inc(wo_hi_done, 1)
                    wait(act, o_in[h % WR], 16 * (n * (H // WR) + h // WR + 1))
                    if is_first(n) and h < 2:
                        act.wait_ge(down_done, G * FT - 1 + h)
                    else:
                        wait(act, proj_used, n * H + h - 1)
                    nc.scalar.activation(o_hi[:, h % 2, :], o_raw[:, h % WR, :], ACT.Copy).then_inc(o_hi_done, 1)
                    if is_first(n) and h == 1:
                        silu_g(G - 1)

            signs(0)
            for j in range(FT):
                if j % WG == 0 and j // WG + 1 < FT // WG:
                    signs(j // WG + 1)
                hidden(0, j)
            with act.Fori(1, G) as n:
                for j in range(FT):
                    hidden(n, j)
                    if j == 1:
                        silu_g(n - 1)
            out_chunk(0)
            with act.Fori(1, G) as n:
                out_chunk(n)

        @block.vector
        def _(dve):
            def split_hidden(n, j):
                i = n * FT + j
                wait(dve, hid_hi_done, i + 1)
                wait(dve, down_done, i - 1)
                nc.vector.tensor_tensor(hid_lo[:, j % 2, :], relu[:, j % 2, :],
                                        hid_hi[:, j % 2, :].bitcast(fp32), ALU.subtract
                                        ).then_inc(hid_lo_done, 1)

            def read_acc(n):
                wait(dve, down_done, (n + 1) * FT)
                wait(dve, g_stored, 16 * n)
                for b in range(BC):
                    nc.vector.tensor_tensor(g_buf[:, b, :], acc[b][:, :], scale_row[:, :], ALU.mult
                                            ).then_inc(acc_read, 1)

            def gate(n):
                wait(dve, proj_used, (n + 1) * H)
                wait(dve, g_res_in, 16 * (n + 1))
                wait(dve, y_stored, 16 * BC * n)
                for b in range(BC):
                    nc.vector.scalar_tensor_tensor(
                        y_out[:, b, :], acc[b][:, :], rms[:, bass.ds(n * BC + b, 1)], g_res[:, b, :],
                        ALU.mult, ALU.mult).then_inc(gated_out, 1)

            def add_x(n):
                wait(dve, x_res_in, 16 * (n + 1))
                for b in range(BC):
                    wait(dve, gated_out, n * BC + b + 1)
                    nc.vector.tensor_tensor(y_out[:, b, :], y_out[:, b, :], x_res[:, b, :], ALU.add
                                            ).then_inc(y_done, 1)

            def out_chunk(n):
                for h in range(H):
                    if is_first(n):
                        dve.wait_ge(wo_hi_done, h + 1)
                        nc.vector.tensor_tensor(wo_lo[:, h, :], wo_raw[:, h % 2, :],
                                                wo_hi[:, h, :].bitcast(fp32), ALU.subtract
                                                ).then_inc(wo_lo_done, 1)
                        if h == 0:
                            read_acc(G - 1)
                    wait(dve, o_hi_done, n * H + h + 1)
                    if is_first(n) and h < 2:
                        dve.wait_ge(down_done, G * FT - 1 + h)
                    else:
                        wait(dve, proj_used, n * H + h - 1)
                    nc.vector.tensor_tensor(o_lo[:, h % 2, :], o_raw[:, h % WR, :],
                                            o_hi[:, h % 2, :].bitcast(fp32), ALU.subtract
                                            ).then_inc(o_lo_done, 1)
                    if is_first(n) and h == 3:
                        dve.wait_ge(sq_total, 1)
                        nc.vector.tensor_scalar(
                            mean_sq[:, :], bank_sq[:, 0:2 * NB].rearrange("p (b r) -> p b r", r=2)[:, :, 0],
                            1.0 / HD, RMS_EPS, ALU.mult, ALU.add).then_inc(mean_done, 1)
                        dve.wait_ge(rms_done, 1)
                    if not is_first(n) and h == 0:
                        gate(n - 1)
                    if not is_first(n) and h == 1:
                        add_x(n - 1)

            dve.wait_ge(scale_in, 32)
            nc.vector.tensor_scalar(scale_row[:, :], scale_row[:, :], out_scale[:, 0:1], None, ALU.mult
                                    ).then_inc(scaled, 1)
            dve.wait_ge(scaled, 1)
            for j in range(FT):
                split_hidden(0, j)
            with dve.Fori(1, G) as n:
                for j in range(FT):
                    if j == 0:
                        read_acc(n - 1)
                    split_hidden(n, j)
            out_chunk(0)
            with dve.Fori(1, G) as n:
                out_chunk(n)
            gate(G - 1)
            add_x(G - 1)

        @block.tensor
        def _(pe):
            def up(n, j):
                i = n * FT + j
                if is_first(n):
                    wait(pe, up_signed, j // WG + 1)
                wait(pe, relu_done, i - 1)
                for k in range(2 * KT):
                    part, t = (x_hi, x_lo)[k // KT], k % KT
                    last = nc.tensor.matmul(up_banks[j % 2][:, :], up_sign[:, t, j * P:(j + 1) * P],
                                            part[:, t, bass.ds(n * CH, CH)],
                                            start=(k == 0), stop=(k == 2 * KT - 1))
                last.then_inc(up_done, 1)

            def down(n, j):
                if is_first(n):
                    wait(pe, down_signed, j // WG + 1)
                wait(pe, hid_lo_done, n * FT + j + 1)
                for b in range(BC):
                    if j == 0:
                        wait(pe, acc_read, (n - 1) * BC + b + 1)
                    for part in (hid_hi, hid_lo):
                        last = nc.tensor.matmul(acc[b][:, :], part[:, j % 2, b * P:(b + 1) * P],
                                                down_sign[:, j, :], start=(j == 0 and part is hid_hi),
                                                stop=(j == FT - 1 and part is hid_lo))
                last.then_inc(down_done, 1)

            def ffn_chunk(n):
                up(n, 0)
                for j in range(FT):
                    if j + 1 < FT:
                        up(n, j + 1)
                    down(n, j)

            def out_chunk(n):
                for h in range(H):
                    if is_first(n):
                        wait(pe, wo_lo_done, h + 1)
                    wait(pe, o_lo_done, n * H + h + 1)
                    for b in range(BC):
                        if h == 0 and is_first(n):
                            wait(pe, acc_read, (G - 1) * BC + b + 1)
                        elif h == 0:
                            wait(pe, gated_out, (n - 1) * BC + b + 1)
                        for k, (part, w) in enumerate(((o_hi, wo_hi), (o_lo, wo_hi), (o_hi, wo_lo))):
                            last = nc.tensor.matmul(acc[b][:, :], part[:, h % 2, b * P:(b + 1) * P],
                                                    w[:, h, :], start=(h == 0 and k == 0),
                                                    stop=(h == H - 1 and k == 2))
                    last.then_inc(proj_used, 1)

            ffn_chunk(0)
            with pe.Fori(1, G) as n:
                ffn_chunk(n)
            pe.wait_ge(ones_set, 1)
            pe.wait_ge(relu_done, G * FT)
            for b in range(NB):
                last = nc.tensor.matmul(bank_sq[:, 2 * b:2 * b + 2], sq_sum[:, b * P:(b + 1) * P],
                                        ones[:, :], start=True, stop=True)
            last.then_inc(sq_total, 1)
            out_chunk(0)
            with pe.Fori(1, G) as n:
                out_chunk(n)


def shape_constants(seq, head, lags):
    import numpy as np

    p = np.arange(128)
    own = p[:, None] - p[None, :]
    after = own + 128
    band = np.arange(128 + lags)[None, :] - p[:, None]
    masks = np.concatenate([
        np.eye(128),
        (own >= 0) & (own < lags),
        (after >= 0) & (after < lags),
        (band >= 0) & (band < lags),
        (p[:, None] % lags) == np.arange(lags)[None, :],
    ], axis=1).astype(np.float32)
    inv = np.float32(1.0) / np.power(np.float32(1e6), np.arange(0, head, 2, dtype=np.float32) / np.float32(head),
                                     dtype=np.float32)
    angle = (inv[:, None] * np.arange(seq, dtype=np.float32)[None, :]).astype(np.float64)
    cos = np.concatenate([np.cos(angle), np.cos(angle)], 0).astype(np.float32)
    sin = np.concatenate([-np.sin(angle), np.sin(angle)], 0).astype(np.float32)
    return masks, cos, sin


def kernel(**inputs):
    import numpy as np
    import concourse.bacc as bacc
    from concourse import mybir
    from concourse.bass_utils import run_bass_kernel_spmd

    given = {n.replace("L0_attn_", "").replace("L0_ffn_", ""): np.asarray(a) for n, a in inputs.items()}
    _, seq, hid = given["x"].shape
    heads = given["Wa"].shape[1]

    def by_tile(a):
        a = a.reshape(a.shape[0] // 128, 128, -1)
        return np.ascontiguousarray(a.transpose(1, 0, 2).reshape(128, -1))

    masks, cos, sin = shape_constants(seq, given["Wq"].shape[1] // heads, 4)
    arrays = {
        "x": given["x"].reshape(seq, hid),
        "wq": given["Wq"], "wk": given["Wk"], "wv": given["Wv"], "wz": given["Wz"],
        "wa": given["Wa"], "wb": given["Wb"],
        "conv_q": by_tile(given["conv_q_w"]), "conv_k": by_tile(given["conv_k_w"]),
        "conv_v": by_tile(given["conv_v_w"]), "norm_w": by_tile(given["norm_w"]),
        "wout": given["Wout"],
        "up_t": np.ascontiguousarray(given["up_weight"].T),
        "down_t": np.ascontiguousarray(given["down_weight"].T),
        "up_scale": by_tile(given["up_scale"]),
        "down_scale": given["down_scale"], "output_scale": given["output_scale"],
        "masks": masks, "rope_cos": cos, "rope_sin": sin,
    }
    nc = bacc.Bacc("TRN2", target_bir_lowering=False, num_devices=1)
    args, feed = {}, {}
    for name, a in arrays.items():
        a = np.ascontiguousarray(a)
        feed[f"in_{name}"] = a
        args[name] = nc.dram_tensor(f"in_{name}", a.shape, mybir.dt.from_np(a.dtype), kind="ExternalInput").ap()
    args["out"] = nc.dram_tensor("out_y", (seq, hid), mybir.dt.float32, kind="ExternalOutput").ap()
    gated_recurrent_block_kernel(nc, **args)
    result = run_bass_kernel_spmd(nc, [feed], core_ids=[0])
    return result.results[0]["out_y"].reshape(1, seq, hid)
```

```python
import concourse.bass as bass
from concourse import mybir
from contextlib import ExitStack


def gated_recurrent_block_kernel(
    nc: bass.Bass,
    x: bass.AP,
    wq: bass.AP,
    wk: bass.AP,
    wv: bass.AP,
    wz: bass.AP,
    wa: bass.AP,
    wb: bass.AP,
    conv_q: bass.AP,
    conv_k: bass.AP,
    conv_v: bass.AP,
    norm_w: bass.AP,
    wout: bass.AP,
    up_t: bass.AP,
    down_t: bass.AP,
    up_scale: bass.AP,
    down_scale: bass.AP,
    output_scale: bass.AP,
    masks: bass.AP,
    rope_cos: bass.AP,
    rope_sin: bass.AP,
    out: bass.AP,
):
    fp32 = mybir.dt.float32
    f32r = mybir.dt.float32r
    ALU = mybir.AluOpType
    ACT = mybir.ActivationFunctionType

    P = 128
    S, HID = x.shape
    KT = HID // P
    HD = wq.shape[1]
    D = P
    H = HD // D
    FH = up_t.shape[1]
    FT = FH // P
    CH = 512
    G = S // CH
    BC = CH // P
    NB = S // P
    LAGS = 4
    HALO = LAGS - 1
    TAPS = 4
    BW = P + LAGS
    AB = 2 * H
    LN_EPS, RMS_EPS, NORM_FLOOR = 1e-5, 1e-6, 1e-24
    SCALE = float(D) ** -0.5

    C_ID, C_SEL, C_HALO, C_BAND, C_PER = 0, P, 2 * P, 3 * P, 3 * P + BW

    o_scratch = nc.dram_tensor("o_scratch", [HD, S], fp32).ap()

    def wait(eng, sem, count):
        if isinstance(count, int) and count <= 0:
            return
        eng.wait_ge(sem, count)

    top = ExitStack()
    with top:
        def sb(name, shape, dt=fp32, at=top):
            return at.enter_context(nc.sbuf_tensor(name, shape, dt))

        def sem(name, at=top):
            return at.enter_context(nc.semaphore(name))

        const = sb("const", [P, masks.shape[1]])
        neg_half = sb("neg_half", [P, 2 * NB])
        x_hi = sb("x_hi", [P, KT, S], f32r)
        x_lo = sb("x_lo", [P, KT, S], f32r)
        sq_sum = sb("sq_sum", [P, S])
        ones = sb("ones", [P, 2])
        ones_set = sem("ones_set")
        o_stored = [sem(f"o_stored{i}") for i in range(2)]
        nw_sb = sb("nw_sb", [P, H])
        us_sb = sb("us_sb", [P, FT])
        WG = 2
        up_raw = sb("up_raw", [P, 2, KT, WG * P])
        down_raw = sb("down_raw", [P, 2, WG, HID])
        up_in = [sem(f"up_in{i}") for i in range(2)]
        down_in = [sem(f"down_in{i}") for i in range(2)]

        def load_ffn_weights(sp, i):
            sp.dma_start(up_raw[:, i % 2, :, :],
                         up_t.rearrange("(t p) n -> p t n", p=P)[:, :, i * WG * P:(i + 1) * WG * P]
                         ).then_inc(up_in[i % 2], 16)
            sp.dma_start(down_raw[:, i % 2, :, :],
                         down_t.rearrange("(j p) n -> p j n", p=P)[:, i * WG:(i + 1) * WG, :]
                         ).then_inc(down_in[i % 2], 16)

        SQ_EARLY = 2 * BC

        def sum_squares(bank, blocks):
            for b in blocks:
                last = nc.tensor.matmul(bank[:, 2 * b:2 * b + 2], sq_sum[:, b * P:(b + 1) * P],
                                        ones[:, :], start=True, stop=True)
            return last

        ident = const[:, C_ID:C_ID + P]
        sel_own = const[:, C_SEL:C_SEL + P]
        sel_next = const[:, C_HALO:C_HALO + P]
        band = const[:, C_BAND:C_BAND + BW]
        period = const[:, C_PER:C_PER + LAGS]

        banks = [top.enter_context(nc.psum_tensor(f"bank{i}", [P, 512], fp32)) for i in range(4)]
        pair = top.enter_context(nc.psum_tensor("bank45", [P, 1024], fp32))
        banks2 = [top.enter_context(nc.psum_tensor(f"bank{i}", [P, 512], fp32)) for i in (6, 7)]

        att = ExitStack()
        with att:
            cw = {n: sb(f"cw_{n}", [P, H * TAPS], at=att) for n in "qkv"}
            gate0 = sb("gate0", [P, NB, H * LAGS], at=att)
            raw = {n: sb(f"raw_{n}", [P, KT, D], at=att) for n in "qkvz"}
            w_hi = {n: sb(f"whi_{n}", [P, KT, D], f32r, at=att) for n in "qkvz"}
            w_lo = {n: sb(f"wlo_{n}", [P, KT, D], f32r, at=att) for n in "qkvz"}
            w_dram = {"q": wq, "k": wk, "v": wv, "z": wz}
            raw_in = {n: sem(f"raw_in_{n}", att) for n in "qkvz"}
            whi_done = {n: sem(f"whi_done_{n}", att) for n in "qkvz"}
            wlo_done = {n: sem(f"wlo_done_{n}", att) for n in "qkvz"}

            def w_slice(n, h):
                return w_dram[n].rearrange("(t p) n -> p t n", p=P)[:, :, bass.ds(h * D, D)]

            attention(nc, locals())

        ffn_and_output(nc, locals())


def attention(nc, env):
    (fp32, f32r, ALU, ACT, P, S, HID, KT, H, D, CH, G, BC, NB, LAGS, HALO, TAPS, BW, AB, SCALE, LN_EPS,
     NORM_FLOOR, sb, sem, wait) = (
        env[n] for n in ("fp32", "f32r", "ALU", "ACT", "P", "S", "HID", "KT", "H", "D", "CH", "G", "BC", "NB",
                         "LAGS", "HALO", "TAPS", "BW", "AB", "SCALE", "LN_EPS", "NORM_FLOOR", "sb", "sem",
                         "wait"))
    (const, neg_half, x_hi, x_lo, sq_sum, ident, sel_own, sel_next, band, period, banks, pair, banks2, cw, gate0,
     raw, w_hi, w_lo, raw_in, whi_done, wlo_done, w_slice, nw_sb, us_sb, o_scratch, up_raw, down_raw, ones,
     ones_set, o_stored) = (
        env[n] for n in ("const", "neg_half", "x_hi", "x_lo", "sq_sum", "ident", "sel_own", "sel_next", "band",
                         "period", "banks", "pair", "banks2", "cw", "gate0", "raw", "w_hi", "w_lo", "raw_in",
                         "whi_done", "wlo_done", "w_slice", "nw_sb", "us_sb", "o_scratch", "up_raw",
                         "down_raw", "ones", "ones_set", "o_stored"))
    sum_squares, SQ_EARLY = env["sum_squares"], env["SQ_EARLY"]
    NC = H * G
    HALF = D // 2
    with ExitStack() as ctx:
        cos = sb("cos", [P, S], at=ctx)
        sin = sb("sin", [P, S], at=ctx)
        u = {n: sb(f"u_{n}", [P, 2, CH + HALO], at=ctx) for n in "qkv"}
        y = {n: sb(f"y_{n}", [P, 2, CH], at=ctx) for n in "qkv"}
        swapped = {n: sb(f"swapped_{n}", [P, 2, CH], at=ctx) for n in "qk"}
        rot = {"q": sb("rot_q", [P, S + LAGS], at=ctx), "k": sb("rot_k", [P, S], at=ctx)}
        norms = sb("norms", [P, 2, 2 * BC], at=ctx)
        rnorm = sb("rnorm", [P, 2, 2 * BC], at=ctx)
        rq_x = sb("rq_x", [P, BC, LAGS], at=ctx)
        rq_parts = sb("rq_parts", [P, (NB + 1), 2, LAGS], f32r, at=ctx)
        sel_r = sb("sel_r", [P, 2, P], f32r, at=ctx)
        gate_k = sb("gate_k", [P, G, BC, LAGS], at=ctx)
        gates = sb("gates", [P, BC, LAGS], at=ctx)
        coef = sb("coef", [P, 2, BC, BW], at=ctx)
        v_tok = sb("v_tok", [P, NB, D], at=ctx)
        z_act = sb("z_act", [P, 2, CH], at=ctx)
        out_sq = sb("out_sq", [P, CH], at=ctx)
        o_buf = sb("o_buf", [P, 2, CH], at=ctx)
        bank_qv, bank_kz = banks[0], banks[1]
        bank_tqv, bank_tk = banks[2], banks[3]
        bank_out, bank_rq = banks2
        scores = pair[:, :].rearrange("p (b n) -> p b n", b=BC)[:, :, 0:BW]

        def flat(t, dims):
            return t if dims == 2 else t.rearrange("p a b -> p (a b)" if dims == 3 else "p a b c -> p (a b c)")

        homes = (flat(up_raw[:, :, :, :], 4), flat(down_raw[:, :, :, :], 4), flat(v_tok[:, :, :], 3),
                 rot["k"][:, :])
        xt = [home.rearrange("p (b d) -> p b d", b=BC) for home in homes]
        spare = flat(coef[:, :, :, :], 4)
        stats = spare[:, 0:6 * NB].rearrange("p (b n) -> p b n", b=NB)
        mean_var = spare[:, 6 * NB:8 * NB].rearrange("p (b n) -> p b n", b=NB)
        rstd = spare[:, 8 * NB:9 * NB]
        ab_raw, ab_hi, ab_lo = raw["z"], w_hi["z"], w_lo["z"]
        ab_t = rot["q"][0:AB, 0:S]
        ab = out_sq[:, :].rearrange("p (b n) -> p b n", b=NB)
        bx = flat(v_tok[:, :, :], 3)[:, 0:(NB + 1) * H * LAGS].rearrange(
            "p (b h r) -> p b h r", b=NB + 1, h=H)
        turn_banks = (banks[2][:, :], banks[3][:, :], pair[:, 0:CH], pair[:, CH:2 * CH])
        ab_banks = (banks2[0][:, :], banks2[1][:, :])
        bank_ab, pick_banks = pair[:, 0:CH], (pair[:, CH:2 * CH], banks2[0][:, :])
        HALF_NB = NB // 2

        const_in = sem("const_in", ctx)
        x_in = [sem(f"x_in{i}", ctx) for i in range(BC + G - 1)]
        small_in = sem("small_in", ctx)
        ab_zeroed = sem("ab_zeroed", ctx)
        root_set = sem("root_set", ctx)
        ab_in = sem("ab_in", ctx)
        stats_done = sem("stats_done", ctx)
        moments = sem("moments", ctx)
        var_eps = sem("var_eps", ctx)
        rstd_done = sem("rstd_done", ctx)
        normed = sem("normed", ctx)
        turned_x = sem("turned_x", ctx)
        hi_done = sem("hi_done", ctx)
        lo_done = sem("lo_done", ctx)
        abw_hi = sem("abw_hi", ctx)
        abw_lo = sem("abw_lo", ctx)
        ab_proj = sem("ab_proj", ctx)
        abt_done = sem("abt_done", ctx)
        ab_turned = sem("ab_turned", ctx)
        ab_done = sem("ab_done", ctx)
        bx_done = sem("bx_done", ctx)
        picked = sem("picked", ctx)
        prod_done = sem("prod_done", ctx)
        tanh_done = sem("tanh_done", ctx)
        gate_done = sem("gate_done", ctx)

        tables_in = sem("tables_in", ctx)
        cleared = sem("cleared", ctx)
        proj_done = {n: sem(f"proj_done_{n}", ctx) for n in "qkvz"}
        silu_done = {n: sem(f"silu_done_{n}", ctx) for n in "qkv"}
        tap_done = {n: sem(f"tap_done_{n}", ctx) for n in "qkv"}
        conv_done = {n: sem(f"conv_done_{n}", ctx) for n in "qkv"}
        rope_done = {n: sem(f"rope_done_{n}", ctx) for n in "qk"}
        swap_in = {n: [sem(f"swap_in_{n}{i}", ctx) for i in range(2)] for n in "qk"}
        turned_qk = sem("turned_qk", ctx)
        turned_v = sem("turned_v", ctx)
        norms_done = sem("norms_done", ctx)
        v_tok_done = sem("v_tok_done", ctx)
        floor_done = sem("floor_done", ctx)
        root_done = sem("root_done", ctx)
        rnorm_done = sem("rnorm_done", ctx)
        rq_spread = sem("rq_spread", ctx)
        rq_done = sem("rq_done", ctx)
        rq_picked = sem("rq_picked", ctx)
        rq_joined = sem("rq_joined", ctx)
        sel_done = sem("sel_done", ctx)
        scores_done = sem("scores_done", ctx)
        gates_done = sem("gates_done", ctx)
        gated = sem("gated", ctx)
        coef_done = sem("coef_done", ctx)
        out_done = sem("out_done", ctx)
        out_sq_done = sem("out_sq_done", ctx)
        z_done = sem("z_done", ctx)
        o_done = sem("o_done", ctx)
        sq_added = sem("sq_added", ctx)
        block = ctx.enter_context(nc.Block())

        def back(h, g, k):
            h2, g2 = (h, g - k) if g >= k else (h - 1, g - k + G)
            if isinstance(h2, int) and not 0 <= h2 < H:
                return None
            return h2, g2

        def schedule(eng, step):
            for h in (0, 1):
                for g in range(G):
                    step(h, g)
            with eng.Fori(2, H - 1) as h:
                for g in range(G):
                    step(h, g)
            for g in range(G):
                step(H - 1, g)
            for g in range(3):
                step(H, g)

        def is_start(h, g):
            return isinstance(h, int) and h == 0 and g == 0

        def is_last(h):
            return isinstance(h, int) and h >= H - 1

        def cols(g):
            return slice(g * CH, (g + 1) * CH)

        @block.sync
        def _(sp):
            def load_x(g):
                sp.dma_start(xt[g], x_view[:, g * BC:(g + 1) * BC, :]).then_inc(x_in[BC + g - 1], 16)

            x_view = env["x"].rearrange("(b p) d -> p b d", p=P)
            for b in range(BC):
                sp.dma_start(xt[0][:, b, :], x_view[:, b, :]).then_inc(x_in[b], 16)
                if b == 0:
                    sp.dma_start(const[:, :], env["masks"]).then_inc(const_in, 16)
            load_x(1)
            wait(sp, ab_zeroed, 1)
            sp.dma_start(ab_raw[:, :, 0:H], env["wa"].rearrange("(t p) n -> p t n", p=P)).then_inc(ab_in, 16)
            sp.dma_start(ab_raw[:, :, H:AB], env["wb"].rearrange("(t p) n -> p t n", p=P)).then_inc(ab_in, 16)
            for n in "qk":
                sp.dma_start(raw[n][:, :, :], w_slice(n, 0)).then_inc(raw_in[n], 16)
            load_x(2)
            load_x(3)
            sp.dma_start(raw["v"][:, :, :], w_slice("v", 0)).then_inc(raw_in["v"], 16)
            for n in "qkv":
                sp.dma_start(cw[n][:, :], env[f"conv_{n}"]).then_inc(small_in, 16)
            sp.dma_start(nw_sb[:, :], env["norm_w"]).then_inc(small_in, 16)
            sp.dma_start(us_sb[:, :], env["up_scale"]).then_inc(small_in, 16)
            sp.dma_start(cos[:, :], env["rope_cos"]).then_inc(tables_in, 16)
            sp.dma_start(sin[:, :], env["rope_sin"]).then_inc(tables_in, 16)
            wait(sp, abw_lo, 1)
            sp.dma_start(raw["z"][:, :, :], w_slice("z", 0)).then_inc(raw_in["z"], 16)
            wait(sp, turned_x, 2 * BC)

            def load_weights(n, h):
                wait(sp, wlo_done[n], h)
                sp.dma_start(raw[n][:, :, :], w_slice(n, h)).then_inc(raw_in[n], 16)

            def step(h, g):
                c = h * G + g
                if not is_last(h):
                    if g == 0:
                        for n in "qkv":
                            load_weights(n, h + 1)
                    if g == 2:
                        load_weights("z", h + 1)
                if not (isinstance(h, int) and h >= H):
                    for n in "qk":
                        wait(sp, conv_done[n], 3 * c + 3)
                        wait(sp, rope_done[n], 3 * (c - 1))
                        for to, frm in ((0, HALF), (HALF, 0)):
                            sp.dma_start(swapped[n][to:to + HALF, g % 2, :], y[n][frm:frm + HALF, g % 2, :]
                                         ).then_inc(swap_in[n][g % 2], 16)
                if at := back(h, g, 3):
                    h3, g3 = at
                    wait(sp, o_done, c - 2)
                    sp.dma_start(o_scratch[bass.ds(h3 * D, D), cols(g3)], o_buf[:, g3 % 2, :]
                                 ).then_inc(o_stored[g3 % 2], 16)

            for i in range(2):
                env["load_ffn_weights"](sp, i)
            schedule(sp, step)

        @block.gpsimd
        def _(pool):
            def root_of_variance(b):
                pool.wait_ge(moments, b + 1)
                nc.gpsimd.tensor_scalar(rstd[:, b:b + 1], mean_var[:, b, 1:2], LN_EPS, None, ALU.add
                                        ).then_inc(var_eps, 1)
                pool.wait_ge(var_eps, b + 1)
                nc.gpsimd.tensor_tensor(rstd[:, b:b + 1], rstd[:, b:b + 1], neg_half[:, b:b + 1], ALU.pow
                                        ).then_inc(rstd_done, 1)

            nc.gpsimd.memset(neg_half[:, :], -0.5).then_inc(root_set, 1)
            nc.gpsimd.memset(ab_raw[:, :, :], 0.0).then_inc(ab_zeroed, 1)
            pool.wait_ge(root_set, 1)
            for b in range(BC):
                root_of_variance(b)
            nc.gpsimd.memset(ones[:, :], 1.0).then_inc(ones_set, 1)
            for n in "qkv":
                nc.gpsimd.memset(u[n][:, 0, 0:HALO], 0.0).then_inc(cleared, 1)
            nc.gpsimd.memset(rot["q"][:, S:S + LAGS], 0.0).then_inc(cleared, 1)
            nc.gpsimd.memset(rq_parts[:, NB, :, :].bitcast(fp32), 0.0).then_inc(cleared, 1)
            nc.gpsimd.memset(sq_sum[:, :], 0.0).then_inc(cleared, 1)
            def split_lo(n, h):
                wait(pool, whi_done[n], h + 1)
                nc.gpsimd.tensor_tensor(w_lo[n][:, :, :], raw[n][:, :, :], w_hi[n][:, :, :].bitcast(fp32),
                                        ALU.subtract).then_inc(wlo_done[n], 1)

            for b in range(BC, NB):
                root_of_variance(b)
                if b == 2 * BC - 1:
                    pool.wait_ge(abw_hi, 1)
                    nc.gpsimd.tensor_tensor(ab_lo[:, :, :], ab_raw[:, :, :], ab_hi[:, :, :].bitcast(fp32),
                                            ALU.subtract).then_inc(abw_lo, 1)
                if b in (BC + 1, 2 * BC + 1, 3 * BC + 1):
                    split_lo("qkv"[b // BC - 1], 0)
            split_lo("z", 0)
            pool.wait_ge(const_in, 16)
            pool.wait_ge(gate_done, 2)

            def step(h, g):
                c = h * G + g
                if at := back(h, g, 1):
                    h1, g1 = at
                    blocks = slice(g1 * BC, (g1 + 1) * BC)
                    wait(pool, floor_done, c)
                    nc.gpsimd.tensor_tensor(rnorm[:, g1 % 2, :], norms[:, g1 % 2, :],
                                            neg_half[:, 0:2 * BC], ALU.pow).then_inc(root_done, 1)
                    wait(pool, root_done, c)
                    wait(pool, rq_done, c - 1)
                    spread = (rnorm[:, g1 % 2, 0:BC][:, :, None].broadcast_to([P, BC, LAGS]),
                              period[:, None, :].broadcast_to([P, BC, LAGS]))
                    nc.gpsimd.tensor_tensor(rq_x[:, :, :], *spread, ALU.mult).then_inc(rq_spread, 1)
                    wait(pool, rq_picked, c - 3)
                    nc.gpsimd.tensor_tensor(rq_parts[:, blocks, 0, :], *spread, ALU.mult).then_inc(rq_spread, 1)
                    wait(pool, rq_spread, 2 * c)
                    nc.gpsimd.tensor_tensor(rq_parts[:, blocks, 1, :], rq_x[:, :, :],
                                            rq_parts[:, blocks, 0, :].bitcast(fp32), ALU.subtract
                                            ).then_inc(rq_done, 1)
                    wait(pool, gates_done, c - 3)
                    nc.gpsimd.tensor_tensor(
                        gate_k[:, g1, :, :], gate0[:, blocks, bass.ds(h1 * LAGS, LAGS)],
                        rnorm[:, g1 % 2, BC:2 * BC][:, :, None].broadcast_to([P, BC, LAGS]),
                        ALU.mult).then_inc(rnorm_done, 1)
                if g == 1 and back(h, g, 0) and not (isinstance(h, int) and h == 0):
                    split_lo("z", h)
                if g == 3 and not is_last(h):
                    for n in "qkv":
                        split_lo(n, h + 1)

            schedule(pool, step)

        @block.scalar
        def _(act):
            def ab_out(g):
                act.wait_ge(ab_proj, g + 1)
                nc.scalar.activation(ab_t[:, g * CH:(g + 1) * CH], ab_banks[g % 2][0:AB, :], ACT.Copy
                                     ).then_inc(abt_done, 1)

            act.wait_ge(const_in, 16)
            nc.scalar.activation(sel_r[:, :, :].rearrange("p a n -> p (a n)"), const[:, P:3 * P], ACT.Copy
                                 ).then_inc(sel_done, 1)
            for b in range(NB):
                if b == BC:
                    act.wait_ge(ab_in, 32)
                    nc.scalar.activation(ab_hi[:, :, :], ab_raw[:, :, :], ACT.Copy).then_inc(abw_hi, 1)
                act.wait_ge(turned_x, b + 1)
                nc.scalar.activation(x_hi[:, :, b * P:(b + 1) * P],
                                     turn_banks[b % 4].rearrange("p (t n) -> p t n", t=KT),
                                     ACT.Copy).then_inc(hi_done, 1)
                if b % 3 == 2 and b // 3 < 3:
                    n = "qkv"[b // 3]
                    act.wait_ge(raw_in[n], 16)
                    nc.scalar.activation(w_hi[n][:, :, :], raw[n][:, :, :], ACT.Copy).then_inc(whi_done[n], 1)
                if b == 3 * BC:
                    ab_out(0)
            ab_out(1)
            act.wait_ge(small_in, 16 * 5)
            act.wait_ge(cleared, 6)

            def split_hi(n, h, c):
                wait(act, raw_in[n], 16 * (h + 1))
                wait(act, proj_done[n], c + 1)
                nc.scalar.activation(w_hi[n][:, :, :], raw[n][:, :, :], ACT.Copy).then_inc(whi_done[n], 1)

            def silu_and_tap(n, bank, h, g, c):
                wait(act, proj_done[n], c + 1)
                wait(act, conv_done[n], 3 * (c - 1))
                nc.scalar.activation(u[n][:, g % 2, HALO:], bank[:, :], ACT.Silu).then_inc(silu_done[n], 1)
                wait(act, conv_done[n], 3 * c)
                wait(act, silu_done[n], 2 * c + 1)
                if n == "v":
                    wait(act, turned_v, c - 1)
                else:
                    wait(act, rope_done[n], 3 * (c - 1))
                    wait(act, turned_qk, c - 1)
                if g < G - 1:
                    nc.scalar.activation(u[n][:, (g + 1) % 2, 0:HALO], bank[:, CH - HALO:CH], ACT.Silu
                                         ).then_inc(silu_done[n], 1)
                else:
                    nc.scalar.activation(u[n][:, 0, 0:HALO], rot["q"][:, S:S + HALO], ACT.Copy
                                         ).then_inc(silu_done[n], 1)
                nc.scalar.activation(y[n][:, g % 2, :], u[n][:, g % 2, 0:CH], ACT.Copy,
                                     scale=cw[n][:, bass.ds(h * TAPS, 1)]).then_inc(tap_done[n], 1)

            silu_and_tap("q", bank_qv, 0, 0, 0)
            silu_and_tap("k", bank_kz, 0, 0, 0)
            ab_out(2)
            ab_out(3)
            act.wait_ge(raw_in["z"], 16)
            nc.scalar.activation(w_hi["z"][:, :, :], raw["z"][:, :, :], ACT.Copy).then_inc(whi_done["z"], 1)

            def step(h, g):
                c = h * G + g
                front = back(h, g, 0)
                if at := back(h, g, 1):
                    g1 = at[1]
                    wait(act, turned_qk, c)
                    wait(act, rnorm_done, c - 2)
                    for i, bank in enumerate((bank_tqv, bank_tk)):
                        for b in range(BC):
                            block_of = bank[:, b * P:(b + 1) * P]
                            last = nc.scalar.activation(block_of, block_of, ACT.Square,
                                                        accum_out=norms[:, g1 % 2, i * BC + b:i * BC + b + 1])
                    last.then_inc(norms_done, 1)
                if front and not is_start(h, g):
                    silu_and_tap("q", bank_qv, h, g, c)
                    silu_and_tap("k", bank_kz, h, g, c)
                if at := back(h, g, 1):
                    g1 = at[1]
                    wait(act, turned_v, c)
                    wait(act, out_done, c - 3)
                    nc.scalar.activation(v_tok[:, g1 * BC:(g1 + 1) * BC, :],
                                         bank_tqv[:, :].rearrange("p (b d) -> p b d", b=BC),
                                         ACT.Copy).then_inc(v_tok_done, 1)
                if g == 3 and not is_last(h):
                    split_hi("q", h + 1, c)
                if front:
                    silu_and_tap("v", bank_qv, h, g, c)
                if g == 3 and not is_last(h):
                    split_hi("k", h + 1, c)
                    split_hi("v", h + 1, c)
                if back(h, g, 3):
                    wait(act, out_done, c - 2)
                    wait(act, sq_added, c - 3)
                    nc.scalar.activation(out_sq[:, :], bank_out[:, :], ACT.Square).then_inc(out_sq_done, 1)
                if is_start(h, g - 1):
                    for i in range(2):
                        part = gate0[:, i * HALF_NB:(i + 1) * HALF_NB, :]
                        act.wait_ge(prod_done, i + 1)
                        nc.scalar.activation(part, part, ACT.Tanh, scale=0.5).then_inc(tanh_done, 1)
                if at := back(h, g, 2):
                    g2 = at[1]
                    wait(act, proj_done["z"], c - 1)
                    wait(act, o_done, c - 3)
                    nc.scalar.activation(z_act[:, g2 % 2, :], bank_kz[:, :], ACT.Silu).then_inc(z_done, 1)
                if g == 1 and front and not (isinstance(h, int) and h == 0):
                    split_hi("z", h, c - 2)

            schedule(act, step)

        @block.vector
        def _(dve):
            def moments_of(b):
                if b < BC:
                    dve.wait_ge(x_in[b], 16)
                elif b % BC == 0:
                    dve.wait_ge(x_in[BC - 1 + b // BC], 16)
                nc.vector.bn_stats(stats[:, b, :], xt[b // BC][:, b % BC, :]).then_inc(stats_done, 1)
                dve.wait_ge(stats_done, b + 1)
                nc.vector.bn_aggr(mean_var[:, b, :], stats[:, b, :]).then_inc(moments, 1)

            def normalize(b):
                part = xt[b // BC][:, b % BC, :]
                dve.wait_ge(rstd_done, b + 1)
                nc.vector.tensor_scalar(part, part, mean_var[:, b, 0:1], rstd[:, b:b + 1],
                                        ALU.subtract, ALU.mult).then_inc(normed, 1)

            def x_low(b):
                dve.wait_ge(hi_done, b + 1)
                nc.vector.tensor_tensor(
                    x_lo[:, :, b * P:(b + 1) * P], turn_banks[b % 4].rearrange("p (t n) -> p t n", t=KT),
                    x_hi[:, :, b * P:(b + 1) * P].bitcast(fp32), ALU.subtract).then_inc(lo_done, 1)

            for b in range(NB + 4):
                if b < NB:
                    moments_of(b)
                if 2 <= b < NB + 2:
                    normalize(b - 2)
                if b >= 4:
                    x_low(b - 4)

            def conv_tap(n, i, h, g, c):
                if i == 1:
                    wait(dve, tap_done[n], c + 1)
                else:
                    wait(dve, conv_done[n], 3 * c + i - 1)
                nc.vector.scalar_tensor_tensor(
                    y[n][:, g % 2, :], u[n][:, g % 2, i:i + CH], cw[n][:, bass.ds(h * TAPS + i, 1)],
                    y[n][:, g % 2, :], ALU.mult, ALU.add).then_inc(conv_done[n], 1)

            def rope(n, i, g, c):
                to, sw = rot[n][:, cols(g)], swapped[n][:, g % 2, :]
                if i == 0:
                    wait(dve, conv_done[n], 3 * c + 3)
                    wait(dve, scores_done, c - 3)
                    op = nc.vector.tensor_tensor(to, y[n][:, g % 2, :], cos[:, cols(g)], ALU.mult)
                elif i == 1:
                    wait(dve, swap_in[n][g % 2], 32 * (c // 2 + 1) if isinstance(c, int) else
                         c * 16 + (32 if g % 2 == 0 else 16))
                    op = nc.vector.tensor_tensor(sw, sw, sin[:, cols(g)], ALU.mult)
                else:
                    wait(dve, rope_done[n], 3 * c + 2)
                    op = nc.vector.tensor_tensor(to, to, sw, ALU.add)
                op.then_inc(rope_done[n], 1)

            def step(h, g):
                c = h * G + g
                if at := back(h, g, 1):
                    g1 = at[1]
                    wait(dve, norms_done, c)
                    nc.vector.tensor_scalar(norms[:, g1 % 2, :], norms[:, g1 % 2, :], NORM_FLOOR, None, ALU.max
                                            ).then_inc(floor_done, 1)
                if back(h, g, 0):
                    for i in (1, 2, 3):
                        conv_tap("q", i, h, g, c)
                        conv_tap("k", i, h, g, c)
                if is_start(h, g):
                    dve.wait_ge(ab_turned, 1)
                    nc.vector.tensor_copy(ab, bank_ab.rearrange("p (b n) -> p b n", b=NB)).then_inc(ab_done, 1)
                    nc.vector.memset(bx[:, NB, :, :], 0.0).then_inc(bx_done, 1)
                    dve.wait_ge(ab_done, 1)
                    dve.wait_ge(const_in, 16)
                    for r in range(LAGS):
                        nc.vector.tensor_scalar(bx[:, 0:NB, :, r], ab[:, :, H:AB], period[:, r:r + 1], None, ALU.mult
                                                ).then_inc(bx_done, 1)
                if is_start(h, g - 1):
                    for i in range(2):
                        blocks = slice(i * HALF_NB, (i + 1) * HALF_NB)
                        dve.wait_ge(picked, i + 1)
                        nc.vector.tensor_tensor(
                            gate0[:, blocks, :].rearrange("p b (h r) -> p b h r", h=H),
                            pick_banks[i].rearrange("p (b h r) -> p b h r", b=HALF_NB, h=H),
                            ab[:, blocks, 0:H][:, :, :, None].broadcast_to([P, HALF_NB, H, LAGS]),
                            ALU.mult).then_inc(prod_done, 1)
                if is_start(h, g):
                    dve.wait_ge(tables_in, 32)
                if back(h, g, 0):
                    conv_tap("v", 1, h, g, c)
                    rope("q", 0, g, c)
                    conv_tap("v", 2, h, g, c)
                    rope("k", 0, g, c)
                    conv_tap("v", 3, h, g, c)
                    for i in (1, 2):
                        rope("q", i, g, c)
                        rope("k", i, g, c)
                if is_start(h, g - 1):
                    for i in range(2):
                        part = gate0[:, i * HALF_NB:(i + 1) * HALF_NB, :]
                        dve.wait_ge(tanh_done, i + 1)
                        nc.vector.tensor_scalar(part, part, 1.0, 0.5 * SCALE, ALU.add, ALU.mult
                                                ).then_inc(gate_done, 1)
                at2, at3 = back(h, g, 2), back(h, g, 3)
                if at2:
                    h2, g2 = at2
                    w = coef[:, g2 % 2, :, :]
                    wait(dve, rq_picked, c - 1)
                    parts = bank_rq[:, 0:2 * BC * LAGS].rearrange("p (b k r) -> p b k r", b=BC, k=2)
                    nc.vector.tensor_reduce(gates[:, :, :], parts.rearrange("p b k r -> p b r k"),
                                            mybir.AxisListType.X, ALU.add).then_inc(rq_joined, 1)
                    wait(dve, rq_joined, c - 1)
                    wait(dve, rnorm_done, c - 1)
                    nc.vector.tensor_tensor(gates[:, :, :], gates[:, :, :], gate_k[:, g2, :, :], ALU.mult
                                            ).then_inc(gates_done, 1)
                    wait(dve, scores_done, c - 1)
                    wait(dve, out_done, c - 2)
                    wait(dve, gates_done, c - 1)
                    nc.vector.tensor_tensor(
                        w.rearrange("p b (a r) -> p b a r", r=LAGS),
                        scores.rearrange("p b (a r) -> p b a r", r=LAGS),
                        gates[:, :, None, :].broadcast_to([P, BC, BW // LAGS, LAGS]),
                        ALU.mult).then_inc(gated, 1)
                if at3:
                    h3, g3 = at3
                    wait(dve, out_sq_done, c - 2)
                    wait(dve, z_done, c - 2)
                    wait(dve, o_stored[g3 % 2], 16 * ((c - 3) // 2) if isinstance(c, int) else
                         8 * (c - 3) - (8 if g3 % 2 else 0))
                    nc.vector.scalar_tensor_tensor(o_buf[:, g3 % 2, :], bank_out[:, :],
                                                   nw_sb[:, bass.ds(h3, 1)], z_act[:, g3 % 2, :],
                                                   ALU.mult, ALU.mult).then_inc(o_done, 1)
                if at2:
                    wait(dve, gated, c - 1)
                    nc.vector.tensor_tensor(w, w, band[:, None, :].broadcast_to([P, BC, BW]), ALU.mult
                                            ).then_inc(coef_done, 1)
                if at3:
                    nc.vector.tensor_tensor(sq_sum[:, cols(g3)], sq_sum[:, cols(g3)], out_sq[:, :], ALU.add
                                            ).then_inc(sq_added, 1)

            schedule(dve, step)

        @block.tensor
        def _(pe):
            def turn_x(b):
                pe.wait_ge(normed, b + 1)
                wait(pe, lo_done, b - 3)
                for t in range(KT):
                    last = nc.tensor.transpose(turn_banks[b % 4][:, t * P:(t + 1) * P],
                                               xt[b // BC][:, b % BC, t * P:(t + 1) * P], ident)
                last.then_inc(turned_x, 1)

            TERMS = 3 * KT

            def project_ab(g, terms=range(TERMS)):
                if terms[0] == 0:
                    pe.wait_ge(abw_lo, 1)
                    pe.wait_ge(lo_done, (g + 1) * BC)
                    wait(pe, abt_done, g - 1)
                for i in terms:
                    w, part = ((ab_hi, x_hi), (ab_lo, x_hi), (ab_hi, x_lo))[i // KT]
                    last = nc.tensor.matmul(ab_banks[g % 2], w[:, i % KT, :], part[:, i % KT, cols(g)],
                                            start=(i == 0), stop=(i == TERMS - 1))
                if terms[-1] == TERMS - 1:
                    last.then_inc(ab_proj, 1)

            def project(n, bank, h, g, c, terms=range(TERMS)):
                if terms[0] == 0:
                    wait(pe, wlo_done[n], h + 1)
                for i in terms:
                    w, part = ((w_hi, x_hi), (w_lo, x_hi), (w_hi, x_lo))[i // KT]
                    last = nc.tensor.matmul(bank[:, :], w[n][:, i % KT, :], part[:, i % KT, cols(g)],
                                            start=(i == 0), stop=(i == TERMS - 1))
                if terms[-1] == TERMS - 1:
                    last.then_inc(proj_done[n], 1)

            pe.wait_ge(const_in, 16)
            for b in range(NB):
                turn_x(b)
                half = range(b % 2 * TERMS // 2, (b % 2 + 1) * TERMS // 2)
                if b // 2 == BC:
                    pe.wait_ge(lo_done, BC)
                    project("q", bank_qv, 0, 0, 0, half)
                elif b // 2 == BC + 1:
                    project_ab(0, half)
                elif b // 2 == BC + 2:
                    project("k", bank_kz, 0, 0, 0, half)
                elif b // 2 == BC + 3:
                    project_ab(1, half)
            project_ab(2)
            project_ab(3)
            pe.wait_ge(cleared, 6)

            def turn_v(g1, c):
                wait(pe, norms_done, c)
                wait(pe, conv_done["v"], 3 * c)
                for b in range(BC):
                    last = nc.tensor.transpose(bank_tqv[:, b * P:(b + 1) * P],
                                               y["v"][:, g1 % 2, b * P:(b + 1) * P], ident)
                last.then_inc(turned_v, 1)

            def sum_values(g3, c):
                wait(pe, coef_done, c - 2)
                wait(pe, v_tok_done, c - 2)
                wait(pe, o_done, c - 3)
                if g3 > 0:
                    nc.tensor.matmul(bank_out[:, 0:LAGS], v_tok[:, g3 * BC - 1, :],
                                     coef[:, (g3 - 1) % 2, BC - 1, P:BW], start=True, stop=False,
                                     skip_group_check=True)
                for b in range(BC):
                    width = BW if b < BC - 1 else P
                    last = nc.tensor.matmul(bank_out[:, b * P:b * P + width], v_tok[:, g3 * BC + b, :],
                                            coef[:, g3 % 2, b, 0:width], start=(b == 0 and g3 == 0),
                                            stop=(b == BC - 1), skip_group_check=True)
                last.then_inc(out_done, 1)

            def step(h, g):
                c = h * G + g
                front = back(h, g, 0)
                at1, at2, at3 = (back(h, g, k) for k in (1, 2, 3))
                if at1:
                    g1 = at1[1]
                    wait(pe, v_tok_done, c - 1)
                    wait(pe, norms_done, c - 1)
                    for n, bank in (("q", bank_tqv), ("k", bank_tk)):
                        wait(pe, conv_done[n], 3 * c)
                        for b in range(BC):
                            last = nc.tensor.transpose(bank[:, b * P:(b + 1) * P],
                                                       y[n][:, g1 % 2, b * P:(b + 1) * P], ident)
                    last.then_inc(turned_qk, 1)
                if front and not is_start(h, g):
                    wait(pe, silu_done["v"], 2 * c)
                    project("q", bank_qv, h, g, c)
                if is_start(h, g - 1):
                    pe.wait_ge(bx_done, LAGS + 1)
                    for i in range(2):
                        own = bx[:, i * HALF_NB:(i + 1) * HALF_NB, :, :].rearrange("p b h r -> p (b h r)")
                        after = bx[:, i * HALF_NB + 1:(i + 1) * HALF_NB + 1, :, :].rearrange(
                            "p b h r -> p (b h r)")
                        nc.tensor.matmul(pick_banks[i], sel_own, own, start=True, stop=False)
                        nc.tensor.matmul(pick_banks[i], sel_next, after, start=False, stop=True
                                         ).then_inc(picked, 1)
                if front and not is_start(h, g):
                    wait(pe, z_done, c - 2)
                    project("k", bank_kz, h, g, c)
                if at1 and front:
                    turn_v(at1[1], c)
                if front:
                    wait(pe, silu_done["q"], 2 * c + 2)
                    project("v", bank_qv, h, g, c)
                if is_start(h, g):
                    pe.wait_ge(abt_done, G)
                    for b in range(NB):
                        last = nc.tensor.transpose(bank_ab[:, b * AB:(b + 1) * AB], ab_t[:, b * P:(b + 1) * P],
                                                   ident[0:AB, 0:AB])
                    last.then_inc(ab_turned, 1)
                if at3 and front:
                    sum_values(at3[1], c)
                if at2:
                    if front:
                        wait(pe, silu_done["k"], 2 * c + 2)
                    else:
                        wait(pe, z_done, c - 2)
                    project("z", bank_kz, at2[0], at2[1], c - 2)
                if at1 and not front:
                    turn_v(at1[1], c)
                if at3 and not front:
                    if not at2:
                        pe.wait_ge(ones_set, 1)
                        pe.wait_ge(sq_added, NC - BC + SQ_EARLY // BC)
                        sum_squares(bank_tk, range(SQ_EARLY))
                    sum_values(at3[1], c)
                if at2:
                    g2 = at2[1]
                    ahead = 1 if g2 < G - 1 else 0
                    wait(pe, rq_done, c - 1 + ahead)
                    wait(pe, gates_done, c - 2)
                    if is_start(h, g - 2):
                        pe.wait_ge(sel_done, 1)
                    own = rq_parts[:, g2 * BC:(g2 + 1) * BC, :, :].rearrange("p b k r -> p (b k r)")
                    after = rq_parts[:, g2 * BC + 1:(g2 + 1) * BC + 1, :, :].rearrange("p b k r -> p (b k r)")
                    nc.tensor.matmul(bank_rq[:, 0:2 * BC * LAGS], sel_r[:, 0, :], own, start=True, stop=False)
                    nc.tensor.matmul(bank_rq[:, 0:2 * BC * LAGS], sel_r[:, 1, :], after, start=False, stop=True
                                     ).then_inc(rq_picked, 1)
                    wait(pe, rope_done["q"], 3 * (c - 1 + ahead))
                    wait(pe, rope_done["k"], 3 * (c - 1))
                    wait(pe, gated, c - 2)
                    for b in range(BC):
                        at = (g2 * BC + b) * P
                        last = nc.tensor.matmul(scores[:, b, :], rot["k"][:, at:at + P], rot["q"][:, at:at + BW],
                                                start=True, stop=True)
                    last.then_inc(scores_done, 1)

            schedule(pe, step)


def ffn_and_output(nc, env):
    (fp32, f32r, ALU, ACT, P, S, HID, KT, H, D, HD, FT, CH, G, BC, NB, RMS_EPS, sb, sem, wait) = (
        env[n] for n in ("fp32", "f32r", "ALU", "ACT", "P", "S", "HID", "KT", "H", "D", "HD", "FT", "CH", "G",
                         "BC", "NB", "RMS_EPS", "sb", "sem", "wait"))
    (neg_half, x_hi, x_lo, sq_sum, us_sb, banks, pair, banks2, o_scratch, WG, up_raw, down_raw, up_in,
     down_in, load_ffn_weights, ones, o_stored) = (
        env[n] for n in ("neg_half", "x_hi", "x_lo", "sq_sum", "us_sb", "banks", "pair", "banks2",
                         "o_scratch", "WG", "up_raw", "down_raw", "up_in", "down_in", "load_ffn_weights",
                         "ones", "o_stored"))
    g_scratch = nc.dram_tensor("g_scratch", [S, HID], fp32).ap().rearrange("(b p) d -> p b d", p=P)
    x_view = env["x"].rearrange("(b p) d -> p b d", p=P)
    out_view = env["out"].rearrange("(b p) d -> p b d", p=P)
    WR = 4
    with ExitStack() as ctx:
        up_sign = sb("up_sign", [P, KT, FT * P], f32r, at=ctx)
        down_sign = sb("down_sign", [P, FT, HID], f32r, at=ctx)
        scale_row = sb("scale_row", [P, HID], at=ctx)
        out_scale = sb("out_scale", [P, 1], at=ctx)
        relu = sb("relu", [P, 2, CH], at=ctx)
        hid_hi = sb("hid_hi", [P, 2, CH], f32r, at=ctx)
        hid_lo = sb("hid_lo", [P, 2, CH], f32r, at=ctx)
        g_buf = sb("g_buf", [P, BC, HID], at=ctx)
        wo_raw = sb("wo_raw", [P, KT, HID], at=ctx)
        o_raw = sb("o_raw", [P, WR, CH], at=ctx)
        mean_sq = sb("mean_sq", [P, NB], at=ctx)
        rms = sb("rms", [P, NB], at=ctx)
        assert H == G * KT and HID == CH

        def wo_tile(part, a, t):
            return part[:, t, bass.ds(a * CH, CH)]

        o_hi, o_lo, y_out = hid_hi, hid_lo, g_buf
        x_res = up_raw[:, :, :, :].rearrange("p a t n -> p (a t n)").rearrange("p (b d) -> p b d", b=BC)
        g_res = down_raw[:, :, :, :].rearrange("p a t n -> p (a t n)").rearrange("p (b d) -> p b d", b=BC)
        up_banks = banks2
        bank_sq = banks[3]
        acc = [bank[:, :] for bank in banks]
        acc_sets = ([pair[:, 0:512], pair[:, 512:1024], banks2[0][:, :], banks2[1][:, :]], acc)

        scale_in = sem("scale_in", ctx)
        scaled = sem("scaled", ctx)
        up_signed = sem("up_signed", ctx)
        down_signed = sem("down_signed", ctx)
        up_done = sem("up_done", ctx)
        relu_done = sem("relu_done", ctx)
        hid_hi_done = sem("hid_hi_done", ctx)
        hid_lo_done = sem("hid_lo_done", ctx)
        down_done = sem("down_done", ctx)
        acc_read = sem("acc_read", ctx)
        g_done = sem("g_done", ctx)
        g_stored = sem("g_stored", ctx)
        wo_in = [sem(f"wo_in{i}", ctx) for i in range(KT)]
        o_in = [sem(f"o_in{i}", ctx) for i in range(WR)]
        wo_hi_done = sem("wo_hi_done", ctx)
        wo_lo_done = sem("wo_lo_done", ctx)
        o_hi_done = sem("o_hi_done", ctx)
        o_lo_done = sem("o_lo_done", ctx)
        sq_total = sem("sq_total", ctx)
        mean_done = sem("mean_done", ctx)
        rms_done = sem("rms_done", ctx)
        proj_used = sem("proj_used", ctx)
        x_res_in = sem("x_res_in", ctx)
        g_res_in = sem("g_res_in", ctx)
        last_done = sem("last_done", ctx)
        y_done = sem("y_done", ctx)
        y_stored = sem("y_stored", ctx)
        block = ctx.enter_context(nc.Block())

        def is_first(n):
            return isinstance(n, int) and n == 0

        wout_at = {2 + 3 * t: t for t in range(KT)}

        def out_chunks(eng, chunk):
            second, first = acc_sets[1], acc_sets[0]
            chunk(0, first, None)
            with eng.Fori(0, G // 2 - 1) as m:
                chunk(2 * m + 1, second, first)
                chunk(2 * m + 2, first, second)
            chunk(G - 1, second, first)

        @block.sync
        def _(sp):
            def load_wout(a):
                for t in range(KT):
                    wait(sp, wo_lo_done, (a - 1) * KT + t + 1)
                    sp.dma_start(wo_raw[:, t, :], env["wout"][bass.ds((a * KT + t) * D, D), :]
                                 ).then_inc(wo_in[t], 16)

            def load_o(n, h):
                sp.dma_start(o_raw[:, h % WR, :], o_scratch[h * D:(h + 1) * D, bass.ds(n * CH, CH)]
                             ).then_inc(o_in[h % WR], 16)

            def store_g(n):
                wait(sp, g_done, (n + 1) * BC)
                sp.dma_start(g_scratch[:, bass.ds(n * BC, BC), :], g_buf[:, :, :]).then_inc(g_stored, 16)

            def store_y(n):
                for b in range(BC):
                    wait(sp, y_done, n * BC + b + 1)
                    sp.dma_start(out_view[:, bass.ds(n * BC + b, 1), :], y_out[:, b:b + 1, :]
                                 ).then_inc(y_stored, 16)

            def out_chunk(n):
                for h in range(H):
                    if not is_first(n) or h >= WR:
                        wait(sp, o_lo_done, n * H + h - WR + 1)
                        load_o(n, h)
                    if h == H // 2:
                        if is_first(n):
                            store_g(G - 1)
                        else:
                            store_y(n - 1)
                    if h == H // 2 + 4:
                        if is_first(n):
                            wait(sp, up_signed, FT // WG)
                            wait(sp, down_signed, FT // WG)
                            wait(sp, g_stored, 16 * G)
                        sp.dma_start(x_res, x_view[:, bass.ds(n * BC, BC), :]).then_inc(x_res_in, 16)
                        sp.dma_start(g_res, g_scratch[:, bass.ds(n * BC, BC), :]).then_inc(g_res_in, 16)

            sp.dma_start(scale_row[:, :], env["down_scale"].partition_broadcast(P)).then_inc(scale_in, 16)
            sp.dma_start(out_scale[:, :], env["output_scale"].partition_broadcast(P)).then_inc(scale_in, 16)
            for i in range(2, FT // WG):
                wait(sp, up_signed, i - 1)
                wait(sp, down_signed, i - 1)
                load_ffn_weights(sp, i)
            load_wout(0)
            for i in range(2):
                sp.wait_ge(o_stored[i], 16 * (H * G) // 2)
            for h in range(WR):
                load_o(0, h)
            with sp.Fori(1, G) as n:
                store_g(n - 1)
                load_wout(n)
            out_chunk(0)
            with sp.Fori(1, G) as n:
                out_chunk(n)
            store_y(G - 1)
            sp.wait_ge(y_stored, 16 * NB)

        @block.gpsimd
        def _(pool):
            pool.wait_ge(mean_done, 1)
            nc.gpsimd.tensor_tensor(rms[:, :], mean_sq[:, :], neg_half[:, 0:NB], ALU.pow).then_inc(rms_done, 1)

        @block.scalar
        def _(act):
            def up_signs(i):
                act.wait_ge(up_in[i % 2], 16 * (i // 2 + 1))
                nc.scalar.activation(up_sign[:, :, i * WG * P:(i + 1) * WG * P], up_raw[:, i % 2, :, :],
                                     ACT.Sign).then_inc(up_signed, 1)

            def down_signs(i):
                act.wait_ge(down_in[i % 2], 16 * (i // 2 + 1))
                nc.scalar.activation(down_sign[:, i * WG:(i + 1) * WG, :], down_raw[:, i % 2, :, :],
                                     ACT.Sign).then_inc(down_signed, 1)

            def wout_hi(a, t):
                nc.scalar.activation(wo_tile(x_hi, a, t), wo_raw[:, t, :], ACT.Copy).then_inc(wo_hi_done, 1)

            def hidden(n, j, wout=None):
                i = n * FT + j
                if wout is not None:
                    wait(act, wo_in[wout], 16 * n)
                wait(act, up_done, i + 1)
                wait(act, hid_lo_done, i - 1)
                nc.scalar.activation(relu[:, j % 2, :], up_banks[j % 2][:, :], ACT.Relu,
                                     scale=us_sb[:, j:j + 1]).then_inc(relu_done, 1)
                wait(act, relu_done, i + 1)
                wait(act, down_done, i - 1)
                nc.scalar.activation(hid_hi[:, j % 2, :], relu[:, j % 2, :], ACT.Copy).then_inc(hid_hi_done, 1)
                if wout is not None:
                    wout_hi(n - 1, wout)

            def silu_g(n, blocks=range(BC)):
                for b in blocks:
                    wait(act, acc_read, n * BC + b + 1)
                    nc.scalar.activation(g_buf[:, b, :], g_buf[:, b, :], ACT.Silu).then_inc(g_done, 1)

            def out_chunk(n):
                for h in range(H):
                    if is_first(n) and BC < h <= BC + KT:
                        act.wait_ge(wo_in[h - BC - 1], 16 * G)
                        act.wait_ge(up_done, G * FT)
                        wout_hi(G - 1, h - BC - 1)
                    wait(act, o_in[h % WR], 16 * (n * (H // WR) + h // WR + 1))
                    if is_first(n) and h < 2:
                        act.wait_ge(down_done, G * FT - 1 + h)
                    else:
                        wait(act, proj_used, n * H + h - 1)
                    nc.scalar.activation(o_hi[:, h % 2, :], o_raw[:, h % WR, :], ACT.Copy).then_inc(o_hi_done, 1)
                    if is_first(n) and 1 <= h <= BC:
                        silu_g(G - 1, [h - 1])

            up_signs(0)
            down_signs(0)
            for j in range(FT):
                more = j % WG == 0 and j // WG + 1 < FT // WG
                if more:
                    up_signs(j // WG + 1)
                hidden(0, j)
                if more:
                    down_signs(j // WG + 1)
            with act.Fori(1, G) as n:
                for j in range(FT):
                    hidden(n, j, wout_at.get(j))
                    if j == 1:
                        silu_g(n - 1)
            out_chunks(act, lambda n, sums, sums_before: out_chunk(n))

        @block.vector
        def _(dve):
            def wout_lo(a, t):
                wait(dve, wo_hi_done, a * KT + t + 1)
                nc.vector.tensor_tensor(wo_tile(x_lo, a, t), wo_raw[:, t, :],
                                        wo_tile(x_hi, a, t).bitcast(fp32), ALU.subtract
                                        ).then_inc(wo_lo_done, 1)

            def split_hidden(n, j):
                i = n * FT + j
                wait(dve, hid_hi_done, i + 1)
                wait(dve, down_done, i - 1)
                nc.vector.tensor_tensor(hid_lo[:, j % 2, :], relu[:, j % 2, :],
                                        hid_hi[:, j % 2, :].bitcast(fp32), ALU.subtract
                                        ).then_inc(hid_lo_done, 1)

            def read_acc(n, blocks=range(BC)):
                wait(dve, down_done, (n + 1) * FT)
                wait(dve, g_stored, 16 * n)
                for b in blocks:
                    nc.vector.tensor_tensor(g_buf[:, b, :], acc[b], scale_row[:, :], ALU.mult
                                            ).then_inc(acc_read, 1)

            def finish(n, b, sums, last=False):
                if last:
                    dve.wait_ge(last_done, b + 1)
                elif b == 0:
                    wait(dve, proj_used, (n + 1) * H)
                if b == 0:
                    wait(dve, g_res_in, 16 * (n + 1))
                    wait(dve, x_res_in, 16 * (n + 1))
                    wait(dve, y_stored, 16 * BC * n)
                nc.vector.scalar_tensor_tensor(
                    y_out[:, b, :], sums[b], rms[:, bass.ds(n * BC + b, 1)], g_res[:, b, :],
                    ALU.mult, ALU.mult).then_inc(acc_read, 1)
                wait(dve, acc_read, (G + n) * BC + b + 1)
                nc.vector.tensor_tensor(y_out[:, b, :], y_out[:, b, :], x_res[:, b, :], ALU.add
                                        ).then_inc(y_done, 1)

            def out_chunk(n, sums, sums_before):
                for h in range(H):
                    if is_first(n) and BC < h <= BC + KT:
                        wout_lo(G - 1, h - BC - 1)
                    wait(dve, o_hi_done, n * H + h + 1)
                    if is_first(n) and h < 2:
                        dve.wait_ge(down_done, G * FT - 1 + h)
                    else:
                        wait(dve, proj_used, n * H + h - 1)
                    nc.vector.tensor_tensor(o_lo[:, h % 2, :], o_raw[:, h % WR, :],
                                            o_hi[:, h % 2, :].bitcast(fp32), ALU.subtract
                                            ).then_inc(o_lo_done, 1)
                    if is_first(n) and 1 <= h <= BC:
                        read_acc(G - 1, [h - 1])
                    if is_first(n) and h == H - 1:
                        dve.wait_ge(rms_done, 1)
                    if not is_first(n) and h < BC:
                        finish(n - 1, h, sums_before)

            dve.wait_ge(scale_in, 32)
            nc.vector.tensor_scalar(scale_row[:, :], scale_row[:, :], out_scale[:, 0:1], None, ALU.mult
                                    ).then_inc(scaled, 1)
            dve.wait_ge(sq_total, 1)
            nc.vector.tensor_scalar(
                mean_sq[:, :], bank_sq[:, 0:2 * NB].rearrange("p (b r) -> p b r", r=2)[:, :, 0],
                1.0 / HD, RMS_EPS, ALU.mult, ALU.add).then_inc(mean_done, 1)
            dve.wait_ge(scaled, 1)
            for j in range(FT):
                split_hidden(0, j)
            with dve.Fori(1, G) as n:
                for j in range(FT):
                    split_hidden(n, j)
                    if j == 0:
                        read_acc(n - 1)
                    if j in wout_at:
                        wout_lo(n - 1, wout_at[j])
            out_chunks(dve, out_chunk)
            for b in range(BC):
                finish(G - 1, b, acc_sets[(G - 1) % 2], last=True)

        @block.tensor
        def _(pe):
            def up(n, j):
                i = n * FT + j
                if is_first(n):
                    wait(pe, up_signed, j // WG + 1)
                wait(pe, relu_done, i - 1)
                for k in range(2 * KT):
                    part, t = (x_hi, x_lo)[k // KT], k % KT
                    last = nc.tensor.matmul(up_banks[j % 2][:, :], up_sign[:, t, j * P:(j + 1) * P],
                                            part[:, t, bass.ds(n * CH, CH)],
                                            start=(k == 0), stop=(k == 2 * KT - 1))
                last.then_inc(up_done, 1)

            def down(n, j):
                if is_first(n):
                    wait(pe, down_signed, j // WG + 1)
                wait(pe, hid_lo_done, n * FT + j + 1)
                for b in range(BC):
                    if j == 0 and is_first(n) and b == 3:
                        pe.wait_ge(mean_done, 1)
                    elif j == 0:
                        wait(pe, acc_read, (n - 1) * BC + b + 1)
                    for part in (hid_hi, hid_lo):
                        last = nc.tensor.matmul(acc[b], part[:, j % 2, b * P:(b + 1) * P],
                                                down_sign[:, j, :], start=(j == 0 and part is hid_hi),
                                                stop=(j == FT - 1 and part is hid_lo))
                last.then_inc(down_done, 1)

            def ffn_chunk(n):
                for j in range(FT):
                    if j + 1 < FT:
                        up(n, j + 1)
                    elif not (isinstance(n, int) and n == G - 1):
                        up(n + 1, 0)
                    down(n, j)

            def project(h, b, sums):
                for k, (part, w) in enumerate(((o_hi, x_hi), (o_lo, x_hi), (o_hi, x_lo))):
                    last = nc.tensor.matmul(sums[b], part[:, h % 2, b * P:(b + 1) * P],
                                            wo_tile(w, h // KT, h % KT),
                                            start=(h == 0 and k == 0), stop=(h == H - 1 and k == 2))
                return last

            def out_chunk(n, sums, sums_before):
                is_final = isinstance(n, int) and n == G - 1
                for h in range(H - 2 if is_final else H):
                    if is_first(n) and (h == 0 or h >= (G - 1) * KT):
                        wait(pe, wo_lo_done, max(h + 1, (G - 1) * KT))
                    wait(pe, o_lo_done, n * H + h + 1)
                    for b in range(BC):
                        if h == 0 and is_first(n) and b >= 2:
                            pe.wait_ge(relu_done, G * FT - 3 + b)
                        elif h == 0 and not is_first(n):
                            wait(pe, acc_read, (G + n - 2) * BC + b + 1)
                        last = project(h, b, sums)
                    last.then_inc(proj_used, 1)
                if is_final:
                    for b, h in ((0, H - 2), (1, H - 2), (0, H - 1), (1, H - 1),
                                 (2, H - 2), (2, H - 1), (3, H - 2), (3, H - 1)):
                        wait(pe, o_lo_done, n * H + h + 1)
                        last = project(h, b, sums)
                        if h == H - 1:
                            last.then_inc(last_done, 1)

            env["sum_squares"](bank_sq, range(env["SQ_EARLY"], NB)).then_inc(sq_total, 1)
            up(0, 0)
            ffn_chunk(0)
            with pe.Fori(1, G - 1) as n:
                ffn_chunk(n)
            ffn_chunk(G - 1)
            out_chunks(pe, out_chunk)


def shape_constants(seq, head, lags):
    import numpy as np

    p = np.arange(128)
    own = p[:, None] - p[None, :]
    after = own + 128
    band = np.arange(128 + lags)[None, :] - p[:, None]
    masks = np.concatenate([
        np.eye(128),
        (own >= 0) & (own < lags),
        (after >= 0) & (after < lags),
        (band >= 0) & (band < lags),
        (p[:, None] % lags) == np.arange(lags)[None, :],
    ], axis=1).astype(np.float32)
    inv = np.float32(1.0) / np.power(np.float32(1e6), np.arange(0, head, 2, dtype=np.float32) / np.float32(head),
                                     dtype=np.float32)
    angle = (inv[:, None] * np.arange(seq, dtype=np.float32)[None, :]).astype(np.float64)
    cos = np.concatenate([np.cos(angle), np.cos(angle)], 0).astype(np.float32)
    sin = np.concatenate([-np.sin(angle), np.sin(angle)], 0).astype(np.float32)
    return masks, cos, sin


def kernel(**inputs):
    import numpy as np
    import concourse.bacc as bacc
    from concourse import mybir
    from concourse.bass_utils import run_bass_kernel_spmd

    given = {n.replace("L0_attn_", "").replace("L0_ffn_", ""): np.asarray(a) for n, a in inputs.items()}
    _, seq, hid = given["x"].shape
    heads = given["Wa"].shape[1]

    def by_tile(a):
        a = a.reshape(a.shape[0] // 128, 128, -1)
        return np.ascontiguousarray(a.transpose(1, 0, 2).reshape(128, -1))

    masks, cos, sin = shape_constants(seq, given["Wq"].shape[1] // heads, 4)
    arrays = {
        "x": given["x"].reshape(seq, hid),
        "wq": given["Wq"], "wk": given["Wk"], "wv": given["Wv"], "wz": given["Wz"],
        "wa": given["Wa"], "wb": given["Wb"],
        "conv_q": by_tile(given["conv_q_w"]), "conv_k": by_tile(given["conv_k_w"]),
        "conv_v": by_tile(given["conv_v_w"]), "norm_w": by_tile(given["norm_w"]),
        "wout": given["Wout"],
        "up_t": np.ascontiguousarray(given["up_weight"].T),
        "down_t": np.ascontiguousarray(given["down_weight"].T),
        "up_scale": by_tile(given["up_scale"]),
        "down_scale": given["down_scale"], "output_scale": given["output_scale"],
        "masks": masks, "rope_cos": cos, "rope_sin": sin,
    }
    nc = bacc.Bacc("TRN2", target_bir_lowering=False, num_devices=1)
    args, feed = {}, {}
    for name, a in arrays.items():
        a = np.ascontiguousarray(a)
        feed[f"in_{name}"] = a
        args[name] = nc.dram_tensor(f"in_{name}", a.shape, mybir.dt.from_np(a.dtype), kind="ExternalInput").ap()
    args["out"] = nc.dram_tensor("out_y", (seq, hid), mybir.dt.float32, kind="ExternalOutput").ap()
    gated_recurrent_block_kernel(nc, **args)
    result = run_bass_kernel_spmd(nc, [feed], core_ids=[0])
    return result.results[0]["out_y"].reshape(1, seq, hid)
```
